# Optimizing a Trainium2 kernel written in Bass

```python
import numpy as np
import jax
import jax.numpy as jnp

def _softmax(x, axis=-1):
    return jax.nn.softmax(x, axis=axis)

def _gelu(x):
    return jax.nn.gelu(x, approximate=True)

def _silu(x):
    return jax.nn.silu(x)

def _sigmoid(x):
    return jax.nn.sigmoid(x)

def _layernorm(x, axis=-1, eps=1e-05):
    m = jnp.mean(x, axis=axis, keepdims=True)
    v = jnp.var(x, axis=axis, keepdims=True)
    return (x - m) / jnp.sqrt(v + eps)

def _scatter_add(tgt, idx, src, axis=0):
    return tgt.at[idx].add(src)

def _segment_sum(src, seg, n):
    return jax.ops.segment_sum(src, seg, n)
kernel_name = 'mk_adj_seq_d1_adj_r2_32b762'

def setup_inputs(seed: int=0):
    np.random.seed(seed)
    _w = jnp.asarray

    def _rec_inputs():
        import jax
        import jax.numpy as jnp
        _gk = jax.random.key(seed)
        x = -0.0005207 + 1.001 * jax.random.normal(jax.random.fold_in(_gk, 1), (32, 256, 256), jnp.float32)
        _w = (1.0 + jnp.arange(256, dtype=jnp.float32)) ** (-0.5)
        _w = _w / _w.mean()
        _pij = jnp.clip(0.0625 * _w[:, None] * _w[None, :], 0.0, 1.0)
        _a = jax.random.uniform(jax.random.fold_in(_gk, 2), (32, 256, 256)) < _pij
        adj = _a
        return (x, adj)
    x, adj = _rec_inputs()

    def _L0_gnn_setup():
        import jax, jax.numpy as jnp
        import numpy as np
        HIDDEN = 256
        HEADS = 8
        HEAD_DIM = HIDDEN // HEADS
        D_FF = 4 * HIDDEN
        NEG = -1000000000.0

        def _layernorm(x, g, b, eps=1e-05):
            mu = jnp.mean(x, axis=-1, keepdims=True)
            var = jnp.var(x, axis=-1, keepdims=True)
            return (x - mu) * jax.lax.rsqrt(var + eps) * g + b
        key = jax.random.key(seed)
        ks = jax.random.split(key, 16)
        B, S = (2, 1024)
        s = 1.0 / np.sqrt(HIDDEN)
        inp = {'x': jax.random.normal(ks[0], (B, S, HIDDEN), dtype=jnp.float32), 'adj_mask': jax.random.bernoulli(ks[1], 0.5, (B, S, S)), 'ln1_g': jnp.ones((HIDDEN,), jnp.float32), 'ln1_b': jnp.zeros((HIDDEN,), jnp.float32), 'ln2_g': jnp.ones((HIDDEN,), jnp.float32), 'ln2_b': jnp.zeros((HIDDEN,), jnp.float32), 'Wq': jax.random.uniform(ks[2], (HIDDEN, HIDDEN), jnp.float32, -s, s), 'bq': jnp.zeros((HIDDEN,), jnp.float32), 'Wk': jax.random.uniform(ks[3], (HIDDEN, HIDDEN), jnp.float32, -s, s), 'bk': jnp.zeros((HIDDEN,), jnp.float32), 'Wv': jax.random.uniform(ks[4], (HIDDEN, HIDDEN), jnp.float32, -s, s), 'bv': jnp.zeros((HIDDEN,), jnp.float32), 'Wo': jax.random.uniform(ks[5], (HIDDEN, HIDDEN), jnp.float32, -s, s), 'bo': jnp.zeros((HIDDEN,), jnp.float32), 'W1': jax.random.uniform(ks[6], (HIDDEN, D_FF), jnp.float32, -s, s), 'b1': jnp.zeros((D_FF,), jnp.float32), 'W2': jax.random.uniform(ks[7], (D_FF, HIDDEN), jnp.float32, -1.0 / np.sqrt(D_FF), 1.0 / np.sqrt(D_FF)), 'b2': jnp.zeros((HIDDEN,), jnp.float32)}
        return inp
    _L0_gnn_all = _L0_gnn_setup()
    _L0_gnn_in = {k: v for k, v in _L0_gnn_all.items() if k in ('ln1_g', 'ln1_b', 'ln2_g', 'ln2_b', 'Wq', 'bq', 'Wk', 'bk', 'Wv', 'bv', 'Wo', 'bo', 'W1', 'b1', 'W2', 'b2')}
    del _L0_gnn_all
    return {'x': x, 'adj': adj, 'L0_gnn_ln1_g': _L0_gnn_in['ln1_g'], 'L0_gnn_ln1_b': _L0_gnn_in['ln1_b'], 'L0_gnn_ln2_g': _L0_gnn_in['ln2_g'], 'L0_gnn_ln2_b': _L0_gnn_in['ln2_b'], 'L0_gnn_Wq': _L0_gnn_in['Wq'], 'L0_gnn_bq': _L0_gnn_in['bq'], 'L0_gnn_Wk': _L0_gnn_in['Wk'], 'L0_gnn_bk': _L0_gnn_in['bk'], 'L0_gnn_Wv': _L0_gnn_in['Wv'], 'L0_gnn_bv': _L0_gnn_in['bv'], 'L0_gnn_Wo': _L0_gnn_in['Wo'], 'L0_gnn_bo': _L0_gnn_in['bo'], 'L0_gnn_W1': _L0_gnn_in['W1'], 'L0_gnn_b1': _L0_gnn_in['b1'], 'L0_gnn_W2': _L0_gnn_in['W2'], 'L0_gnn_b2': _L0_gnn_in['b2']}

def reference(x, adj, L0_gnn_ln1_g, L0_gnn_ln1_b, L0_gnn_ln2_g, L0_gnn_ln2_b, L0_gnn_Wq, L0_gnn_bq, L0_gnn_Wk, L0_gnn_bk, L0_gnn_Wv, L0_gnn_bv, L0_gnn_Wo, L0_gnn_bo, L0_gnn_W1, L0_gnn_b1, L0_gnn_W2, L0_gnn_b2):
    import jax
    import jax.numpy as jnp

    def _L0_gnn_ref(x, adj_mask, ln1_g, ln1_b, ln2_g, ln2_b, Wq, bq, Wk, bk, Wv, bv, Wo, bo, W1, b1, W2, b2):
        import jax, jax.numpy as jnp
        import numpy as np
        HIDDEN = 256
        HEADS = 8
        HEAD_DIM = HIDDEN // HEADS
        D_FF = 4 * HIDDEN
        NEG = -1000000000.0

        def _layernorm(x, g, b, eps=1e-05):
            mu = jnp.mean(x, axis=-1, keepdims=True)
            var = jnp.var(x, axis=-1, keepdims=True)
            return (x - mu) * jax.lax.rsqrt(var + eps) * g + b
        B, S, H = x.shape
        nx = _layernorm(x, ln1_g, ln1_b)
        q = (nx @ Wq + bq).reshape(B, S, HEADS, HEAD_DIM)
        k = (nx @ Wk + bk).reshape(B, S, HEADS, HEAD_DIM)
        v = (nx @ Wv + bv).reshape(B, S, HEADS, HEAD_DIM)
        scores = jnp.einsum('bqhd,bkhd->bhqk', q, k) / np.sqrt(HEAD_DIM)
        scores = jnp.where(adj_mask[:, None, :, :], scores, NEG)
        attn = jax.nn.softmax(scores, axis=-1)
        out = jnp.einsum('bhqk,bkhd->bqhd', attn, v).reshape(B, S, H)
        out = out @ Wo + bo
        x = x + out
        nx = _layernorm(x, ln2_g, ln2_b)
        mlp = jax.nn.gelu(nx @ W1 + b1, approximate=False) @ W2 + b2
        return x + mlp
    x = _L0_gnn_ref(x, adj, L0_gnn_ln1_g, L0_gnn_ln1_b, L0_gnn_ln2_g, L0_gnn_ln2_b, L0_gnn_Wq, L0_gnn_bq, L0_gnn_Wk, L0_gnn_bk, L0_gnn_Wv, L0_gnn_bv, L0_gnn_Wo, L0_gnn_bo, L0_gnn_W1, L0_gnn_b1, L0_gnn_W2, L0_gnn_b2)
    return x

_drawn_inputs = setup_inputs


def setup_inputs(seed=0):
    import zlib

    import numpy as np

    out = dict(_drawn_inputs(seed))
    spreads = {'L0_gnn_ln1_g': (1.0, 0.6),
     'L0_gnn_ln1_b': (0.0, 0.1),
     'L0_gnn_ln2_g': (1.0, 0.2),
     'L0_gnn_ln2_b': (0.0, 0.381),
     'L0_gnn_bq': (0.0, 0.8),
     'L0_gnn_bk': (0.0, 0.8),
     'L0_gnn_bv': (0.0, 0.1),
     'L0_gnn_bo': (0.0, 0.1),
     'L0_gnn_b1': (0.0, 0.1),
     'L0_gnn_b2': (0.0, 0.1)}
    factors = {}
    for name, (base, spread) in spreads.items():
        noise = np.random.default_rng([zlib.crc32(name.encode()), seed]).standard_normal(out[name].shape)
        drawn = base * np.exp(spread * noise) if base else spread * noise
        out[name] = jnp.asarray(drawn.astype(out[name].dtype))
    for name, factor in factors.items():
        out[name] = (out[name] * factor).astype(out[name].dtype)
    return out
```

```python
from contextlib import ExitStack

import concourse.bass as bass
from concourse import mybir

ALU = mybir.AluOpType
ACT = mybir.ActivationFunctionType
AX = mybir.AxisListType
F32 = mybir.dt.float32
F32R = mybir.dt.float32r
U8 = mybir.dt.uint8

P = 128
HEADS = 8
LN_EPS = 1e-5
MASKED = 1e30
HUGE = 3e38

DENSE_UNITS = (
    ["W2_0", "RT0", "W2_1", "RT1", "RT2", "LN1T0", "LN1T1", "QK0", "QK1", "RT3"]
    + ["Wo0", "QK2", "Wo1", "QK3", "V0", "V1", "LN2T0", "LN2T1"]
    + [f"W1_{f}" for f in range(8)]
)
DENSE_BANKS = 3
COPIED_BY_ACT = (0, 3, 6, 8, 11, 14)
STEPS = 16


class Plan:

    def __init__(self, groups):
        self.groups = groups
        self.looped = (3, groups - 1)

    def has(self, j, back):
        return not isinstance(j, int) or 0 <= j - back < self.groups

    def units(self, j):
        def there(name):
            if name.startswith("W2"):
                return self.has(j, 2)
            if name[:2] in ("RT", "Wo", "W1") or name.startswith("LN2"):
                return self.has(j, 1)
            return self.has(j, 0)

        return [n for n in DENSE_UNITS if there(n)]

    def bank(self, name):
        return DENSE_UNITS.index(name) % DENSE_BANKS

    def uses(self, j, name, back=0):
        bank = self.bank(name)

        def in_iteration(k):
            return sum(self.bank(n) == bank for n in self.units(k))

        def before(k):
            return sum(in_iteration(i) for i in range(k))

        first = self.looped[0]
        units = self.units(j - back if isinstance(j, int) else first)
        here = sum(self.bank(n) == bank for n in units[: units.index(name) + 1])
        if isinstance(j, int):
            return before(j - back) + here
        each = in_iteration(first)
        return j * each + (before(first) + here - each * (first + back))


def wait(engine, semaphore, count):
    if isinstance(count, int) and count <= 0:
        return
    engine.wait_ge(semaphore, count)


def copied(step, by_act):
    return sum((s in COPIED_BY_ACT) == by_act for s in range(step + 1))


def gnn_block(nc, x, adj, columns, bo_row, b2_row, wq, wk, wv, wo, w1, w2, out):
    B, S, H = x.shape
    FF = w1.shape[1]
    HD = H // HEADS
    KC = H // P
    FC = FF // P
    GB = 2
    G = B // GB
    QT = S // P
    TOK = GB * S
    TILES = TOK // P
    QUADS = GB * KC
    assert (KC, FC, QT, HD, STEPS) == (2, 8, 2, 32, GB * HEADS)
    plan = Plan(G)
    SCALE = float(HD) ** -0.5
    STACK_DMAS = 2 * 4 * 4

    x_dram = x.rearrange("b (t p) h -> p (b t) h", p=P)
    out_dram = out.rearrange("b (t p) h -> p (b t) h", p=P)
    adj_dram = adj.rearrange("b (t p) k -> p (b t) k", p=P)

    with ExitStack() as ctx:
        def sb(name, shape, dt=F32):
            return ctx.enter_context(nc.sbuf_tensor(name, shape, dt))

        def psum(name):
            return ctx.enter_context(nc.psum_tensor(name, [P, 512], F32))

        def sem(name):
            return ctx.enter_context(nc.semaphore(name))

        split = {}
        for name, chunks, width in (("wq", KC, H), ("wk", KC, H), ("wv", KC, H), ("wo", KC, H),
                                    ("w1", KC, FF), ("w2", FC, H)):
            split[name] = (sb(f"{name}_hi", [P, chunks, width], F32R), sb(f"{name}_lo", [P, chunks, width], F32R))
        cols = sb("cols", [P, columns.shape[1]])
        qk_bias = sb("qk_bias", [P, 4])
        bv_col = sb("bv_col", [P, KC])
        b1_col = sb("b1_col", [P, FC])
        bo_all = sb("bo_all", [P, H])
        b2_all = sb("b2_all", [P, H])
        ident = sb("ident", [P, P])
        neg_half = sb("neg_half", [P, TILES])

        norm1 = sb("norm1", [P, TILES, H])
        norm_hi = sb("norm_hi", [P, KC, TOK], F32R)
        norm_lo = sb("norm_lo", [P, KC, TOK], F32R)
        proj_hi = sb("proj_hi", [P, 4, TOK], F32R)
        proj_lo = sb("proj_lo", [P, 4, TOK], F32R)
        q_stack = sb("q_stack", [P, HEADS, TOK], F32R)
        k_stack = sb("k_stack", [P, HEADS, TOK], F32R)
        v_nat = sb("v_nat", [P, GB, QT, H])
        adj_u8 = sb("adj_u8", [P, TILES, S], U8)
        mask_add = sb("mask_add", [P, TILES, S])
        neg_max = sb("neg_max", [P, STEPS, QT])
        row_sum = sb("row_sum", [P, STEPS, QT])
        row_inv = sb("row_inv", [P, 4, QT])
        inv_wide = sb("inv_wide", [P, QT, 4, HD])
        probs = sb("probs", [P, 4, QT, S])
        probs_t = sb("probs_t", [P, 8, 512])
        inv_t = sb("inv_t", [P, 2, S])
        attn = sb("attn", [P, 2, S])
        attn_hi = sb("attn_hi", [P, KC, TOK], F32R)
        attn_lo = sb("attn_lo", [P, KC, TOK], F32R)
        x_mid = sb("x_mid", [P, TILES, H])
        norm2 = sb("norm2", [P, TILES, H])
        result = sb("result", [P, TILES, H])
        hidden = sb("hidden", [P, 2, TOK])
        hid_hi = sb("hid_hi", [P, FC, TOK], F32R)
        hid_lo = sb("hid_lo", [P, FC, TOK], F32R)
        stats1 = sb("stats1", [P, TILES, 6])
        stats2 = sb("stats2", [P, TILES, 6])
        moments1 = sb("moments1", [P, TILES, 2])
        moments2 = sb("moments2", [P, TILES, 2])
        var1 = sb("var1", [P, TILES])
        var2 = sb("var2", [P, TILES])
        rstd1 = sb("rstd1", [P, TILES])
        rstd2 = sb("rstd2", [P, TILES])

        raw = {
            "wq": probs[:, 0].rearrange("p a b -> p (a b)").rearrange("p (c n) -> p c n", c=KC),
            "wk": probs[:, 1].rearrange("p a b -> p (a b)").rearrange("p (c n) -> p c n", c=KC),
            "wv": probs[:, 2].rearrange("p a b -> p (a b)").rearrange("p (c n) -> p c n", c=KC),
            "wo": probs[:, 3].rearrange("p a b -> p (a b)").rearrange("p (c n) -> p c n", c=KC),
            "w1": probs_t[:, 0:4].rearrange("p a b -> p (a b)").rearrange("p (c n) -> p c n", c=KC),
            "w2": probs_t[:, 4:8].rearrange("p a b -> p (a b)").rearrange("p (c n) -> p c n", c=FC),
        }
        G1, BE1, G2, BE2, BQ, BK, BV, B1 = 0, 2, 4, 6, 8, 10, 12, 14

        score_bank = [psum(f"score_bank{i}") for i in range(2)]
        pt_bank = [psum(f"pt_bank{i}") for i in range(2)]
        pv_bank = psum("pv_bank")
        dense = [psum(f"dense{i}") for i in range(DENSE_BANKS)]

        consts_in = sem("consts_in")
        passed = sem("passed")
        w_in = {name: sem(f"{name}_in") for name in split}
        ident_ready, half_ready = sem("ident_ready"), sem("half_ready")
        bias_mm, biases_ready, bv_ready, bv_spread = (
            sem("bias_mm"), sem("biases_ready"), sem("bv_ready"), sem("bv_spread"))
        hi_by_dve, hi_by_act, weights_split = sem("hi_by_dve"), sem("hi_by_act"), sem("weights_split")
        x_ln1_in, x_mid_in, adj_in = sem("x_ln1_in"), sem("x_mid_in"), sem("adj_in")
        stats1_step, moments1_ready, var1_ready, rstd1_ready = (
            sem("stats1_step"), sem("moments1_ready"), sem("var1_ready"), sem("rstd1_ready"))
        stats2_step, moments2_ready, var2_ready, rstd2_ready = (
            sem("stats2_step"), sem("moments2_ready"), sem("var2_ready"), sem("rstd2_ready"))
        norm1_ready, norm2_ready = sem("norm1_ready"), sem("norm2_ready")
        norm1_hi_ready, norm2_hi_ready = sem("norm1_hi_ready"), sem("norm2_hi_ready")
        proj_hi_ready = sem("proj_hi_ready")
        stacked = [sem(f"stacked{c}") for c in range(KC)]
        mask_ready = sem("mask_ready")
        scores_ready, max_ready, probs_ready = sem("scores_ready"), sem("max_ready"), sem("probs_ready")
        pt_filled, pt_by_act, pt_by_dve = sem("pt_filled"), sem("pt_by_act"), sem("pt_by_dve")
        inv_ready, wide_ready = sem("inv_ready"), sem("wide_ready")
        pv_done, attn_ready, attn_hi_ready, attn_lo_ready = (
            sem("pv_done"), sem("attn_ready"), sem("attn_hi_ready"), sem("attn_lo_ready"))
        x_biased, result_seeded = sem("x_biased"), sem("result_seeded")
        hid_hi_ready, hid_lo_ready = sem("hid_hi_ready"), sem("hid_lo_ready")
        stored = sem("stored")
        filled = [sem(f"filled{i}") for i in range(DENSE_BANKS)]
        read = [sem(f"read{i}") for i in range(DENSE_BANKS)]

        def run(engine, body, first=0):
            lo, hi = plan.looped
            for j in range(first, lo):
                body(j)
            with engine.Fori(lo, hi) as j:
                body(j)
            for j in range(hi, G + 2):
                body(j)

        def carried(engine):
            engine.sem_inc(passed, 1)

        def wait_filled(engine, j, unit, back=0):
            wait(engine, filled[plan.bank(unit)], plan.uses(j, unit, back))

        def wait_free(engine, j, unit):
            wait(engine, read[plan.bank(unit)], plan.uses(j, unit) - 1)

        def wait_read(engine, j, unit, back=0):
            wait(engine, read[plan.bank(unit)], plan.uses(j, unit, back))

        def bank_of(unit):
            return dense[plan.bank(unit)]

        block = ctx.enter_context(nc.Block())

        @block.sync
        def _(sp):
            sp.dma_start(cols[:], columns).then_inc(consts_in, 16)
            sp.dma_start(bo_all[:], bo_row.partition_broadcast(P)).then_inc(consts_in, 16)
            sp.dma_start(b2_all[:], b2_row.partition_broadcast(P)).then_inc(consts_in, 16)
            sp.dma_start(norm1[:], x_dram[:, 0:TILES]).then_inc(x_ln1_in, 16)
            for name, w in (("wq", wq), ("wk", wk), ("wv", wv), ("wo", wo), ("w1", w1), ("w2", w2)):
                sp.dma_start(raw[name], w.rearrange("(c p) n -> p c n", p=P)).then_inc(w_in[name], 16)

            def body(j):
                if plan.has(j, 1):
                    wait(sp, norm2_ready, TILES * (j - 1))
                    wait(sp, result_seeded, j - 1)
                    carried(sp)
                    sp.dma_start(x_mid[:], x_dram[:, bass.ds((j - 1) * TILES, TILES)]).then_inc(x_mid_in, 16)
                if plan.has(j, 0):
                    wait(sp, mask_ready, j)
                    carried(sp)
                    sp.dma_start(adj_u8[:], adj_dram[:, bass.ds(j * TILES, TILES)]).then_inc(adj_in, 16)
                if plan.has(j, 2):
                    for u in range(GB):
                        wait_read(sp, j, f"W2_{u}")
                        carried(sp)
                        sp.dma_start(out_dram[:, bass.ds((j - 2) * TILES + QT * u, QT)],
                                     result[:, QT * u:QT * u + QT]).then_inc(stored, 16)
                if plan.has(j, -1):
                    wait_filled(sp, j, "LN1T1")
                    carried(sp)
                    sp.dma_start(norm1[:], x_dram[:, bass.ds((j + 1) * TILES, TILES)]).then_inc(x_ln1_in, 16)
                if plan.has(j, 0):
                    wait(sp, scores_ready, STEPS * j)
                    carried(sp)
                    for c in range(KC):
                        for m, stack, hi_rows, lo_rows in ((2 * c, q_stack, (0, 1), (2, 3)),
                                                           (2 * c + 1, k_stack, (0, 2), (1, 3))):
                            for part, rows in ((proj_hi, hi_rows), (proj_lo, lo_rows)):
                                if part is proj_hi:
                                    wait(sp, proj_hi_ready, 4 * j + m + 1)
                                else:
                                    wait_read(sp, j, f"QK{m}")
                                for r in rows:
                                    for g in range(4):
                                        sp.dma_start(stack[HD * r:HD * r + HD, 4 * c + g].bitcast(F32),
                                                     part[HD * g:HD * g + HD, m].bitcast(F32)).then_inc(stacked[c], 16)

            run(sp, body)
            sp.wait_ge(stored, 16 * GB * G)

        @block.tensor
        def _(pe):
            def beta_products(bank, names, beta):
                column = 0
                for name in names:
                    pe.wait_ge(w_in[name], 16)
                    for m in range(split[name][0].shape[2] // P):
                        for k in range(KC):
                            last = pe.matmul(bank[:, column:column + 1], raw[name][:, k, P * m:P * m + P],
                                             cols[:, beta + k:beta + k + 1], start=(k == 0), stop=(k == KC - 1))
                        column += 1
                last.then_inc(bias_mm, 1)

            pe.wait_ge(consts_in, 16 * 3)
            beta_products(pv_bank, ("wq", "wk", "wv"), BE1)
            pe.wait_ge(ident_ready, 2)

            def three(bank, lhs, rhs, chunks, release=None):
                n = 0
                for c in range(chunks):
                    for a, b in ((0, 0), (0, 1), (1, 0)):
                        last = pe.matmul(bank, lhs(a, c), rhs(b, c), start=(n == 0), stop=(n == 3 * chunks - 1))
                        n += 1
                if release is not None:
                    last.then_inc(release, 1)

            norm = (norm_hi, norm_lo)
            att = (attn_hi, attn_lo)
            hid = (hid_hi, hid_lo)

            def scores(j, t):
                a, b, h = j - 1, t // HEADS, t % HEADS
                if t in (0, 4):
                    wait(pe, stacked[t // 4], 16 * STACK_DMAS * (a + 1))
                wait(pe, max_ready, 2 * (STEPS * a + t - 1))
                for q in range(QT):
                    last = pe.matmul(score_bank[t % 2][:, S * q:S * q + S],
                                     q_stack[:, h, S * b + P * q:S * b + P * q + P],
                                     k_stack[:, h, S * b:S * b + S], start=True, stop=True)
                last.then_inc(scores_ready, 1)

            def turn(j, t):
                a = j - 1
                wait(pe, probs_ready, 2 * (STEPS * a + t + 1))
                before, turns = (t - 2, a) if t >= 2 else (t - 2 + STEPS, a - 1)
                if before in COPIED_BY_ACT:
                    wait(pe, pt_by_act, turns * copied(STEPS - 1, True) + copied(before, True))
                else:
                    wait(pe, pt_by_dve, turns * copied(STEPS - 1, False) + copied(before, False))
                for k in range(QT):
                    for q in range(QT):
                        last = pe.transpose(pt_bank[t % 2][:, S * k + P * q:S * k + P * q + P],
                                            probs[:, t % 4, q, P * k:P * k + P], ident[:])
                last.then_inc(pt_filled, 1)

            def values(j, quad):
                a, b, c = j - 1, quad // KC, quad % KC
                if quad == 0:
                    wait_read(pe, j, "V0", back=1)
                    wait_read(pe, j, "V1", back=1)
                last_step = 4 * quad + 3
                wait(pe, pt_by_act, a * copied(STEPS - 1, True) + copied(last_step, True))
                wait(pe, pt_by_dve, a * copied(STEPS - 1, False) + copied(last_step, False))
                wait(pe, attn_ready, QUADS * a + quad)
                for k in range(QT):
                    for g in range(4):
                        h = 4 * c + g
                        last = pe.matmul(pv_bank[HD * g:HD * g + HD, S * (quad % 2):S * (quad % 2) + S],
                                         v_nat[:, b, k, HD * h:HD * h + HD],
                                         probs_t[:, (4 * quad + g) % 8, S * k:S * k + S],
                                         start=(k == 0), stop=(k == QT - 1))
                last.then_inc(pv_done, 1)

            def turn_inverse(j, quad):
                unit = f"RT{quad}"
                wait(pe, wide_ready, QUADS * (j - 1) + quad + 1)
                wait_free(pe, j, unit)
                for q in range(QT):
                    last = pe.transpose(bank_of(unit)[:, P * q:P * q + P],
                                        inv_wide[:, q].rearrange("p g d -> p (g d)"), ident[:])
                last.then_inc(filled[plan.bank(unit)], 1)

            def mlp_out(j, half, piece):
                unit = f"W2_{half}"
                if piece == 0:
                    wait_free(pe, j, unit)
                if half == 0:
                    wait(pe, hid_hi_ready, FC * (j - 2) + piece + 1)
                    wait(pe, hid_lo_ready, FC * (j - 2) + piece + 1)
                for u in range(QT):
                    tile = QT * half + u
                    for n, (a, b) in enumerate(((0, 0), (0, 1), (1, 0))):
                        last = pe.matmul(bank_of(unit)[:, H * u:H * u + H], hid[a][:, piece, P * tile:P * tile + P],
                                         split["w2"][b][:, piece, :], start=(piece == 0 and u == 0 and n == 0),
                                         stop=(piece == FC - 1 and n == 2), skip_group_check=True)
                if piece == FC - 1:
                    last.then_inc(filled[plan.bank(unit)], 1)

            def turn_norm(j, which, k):
                unit = f"LN{which}T{k}"
                source, ready, group = (norm1, norm1_ready, j) if which == 1 else (norm2, norm2_ready, j - 1)
                wait_free(pe, j, unit)
                for t in range(TILES):
                    if k == 0:
                        wait(pe, ready, TILES * group + t + 1)
                    last = pe.transpose(bank_of(unit)[:, P * t:P * t + P], source[:, t, P * k:P * k + P], ident[:])
                last.then_inc(filled[plan.bank(unit)], 1)

            def project(j, m):
                unit, w = f"QK{m}", split["wk" if m % 2 else "wq"]
                if m == 0:
                    wait_read(pe, j, "LN1T0")
                    wait_read(pe, j, "LN1T1")
                wait_free(pe, j, unit)
                c = m // 2
                three(bank_of(unit)[:], lambda a, k: w[a][:, k, P * c:P * c + P], lambda b, k: norm[b][:, k, :],
                      KC, filled[plan.bank(unit)])

            def project_v(j, b):
                unit = f"V{b}"
                wait_free(pe, j, unit)
                for t in range(QT):
                    tile = QT * b + t
                    three(bank_of(unit)[:, H * t:H * t + H], lambda a, k: norm[a][:, k, P * tile:P * tile + P],
                          lambda c, k: split["wv"][c][:, k, :], KC, filled[plan.bank(unit)] if t == QT - 1 else None)

            def project_out(j, b):
                unit = f"Wo{b}"
                done = QUADS * (j - 1) + KC * (b + 1)
                wait(pe, attn_hi_ready, done)
                wait(pe, attn_lo_ready, done)
                wait_free(pe, j, unit)
                for t in range(QT):
                    tile = QT * b + t
                    three(bank_of(unit)[:, H * t:H * t + H], lambda a, k: att[a][:, k, P * tile:P * tile + P],
                          lambda c, k: split["wo"][c][:, k, :], KC, filled[plan.bank(unit)] if t == QT - 1 else None)

            def mlp_in(j, f):
                unit, w = f"W1_{f}", split["w1"]
                if f == 0:
                    wait_read(pe, j, "LN2T0")
                    wait_read(pe, j, "LN2T1")
                wait_free(pe, j, unit)
                three(bank_of(unit)[:], lambda a, k: w[a][:, k, P * f:P * f + P], lambda b, k: norm[b][:, k, :],
                      KC, filled[plan.bank(unit)])

            def body(j):
                now, before, two_before = plan.has(j, 0), plan.has(j, 1), plan.has(j, 2)
                if isinstance(j, int) and j == 0:
                    pe.wait_ge(weights_split, 3)
                if isinstance(j, int) and j == 1:
                    beta_products(score_bank[0], ("w1",), BE2)
                    pe.wait_ge(w_in["wo"], 16)
                    pe.wait_ge(bv_spread, 1)
                    for k in range(KC):
                        last = pe.matmul(score_bank[1][:, 0:H], inv_t[:, 0, P * k:P * k + P], raw["wo"][:, k, :],
                                         start=(k == 0), stop=(k == KC - 1))
                    last.then_inc(bias_mm, 1)
                    pe.wait_ge(biases_ready, 3)
                    pe.wait_ge(weights_split, 6)
                for t in range(STEPS):
                    if before:
                        scores(j, t)
                        if t % 4 == 2 and t > 2:
                            turn_inverse(j, (t - 6) // 4)
                    if two_before:
                        mlp_out(j, t // 8, t % 8)
                    if before:
                        if t >= 2:
                            turn(j, t - 2)
                        if t % 4 == 3 and t > 3:
                            values(j, (t - 7) // 4)
                if before:
                    turn(j, 14)
                if now:
                    turn_norm(j, 1, 0)
                    turn_norm(j, 1, 1)
                if before:
                    turn(j, 15)
                if now:
                    project(j, 0)
                    project(j, 1)
                if before:
                    turn_inverse(j, 3)
                    values(j, 3)
                    project_out(j, 0)
                if now:
                    project(j, 2)
                if before:
                    project_out(j, 1)
                if now:
                    project(j, 3)
                    project_v(j, 0)
                    project_v(j, 1)
                if before:
                    turn_norm(j, 2, 0)
                    turn_norm(j, 2, 1)
                    for f in range(FC):
                        mlp_in(j, f)

            run(pe, body)

        @block.scalar
        def _(act):
            for name in ("wo", "w2"):
                act.wait_ge(w_in[name], 16)
                nc.scalar.copy(split[name][0][:], raw[name]).then_inc(hi_by_act, 1)

            def exps(j, t):
                a = j - 1
                for q in range(QT):
                    wait(act, max_ready, 2 * (STEPS * a + t) + q + 1)
                    nc.scalar.activation(probs[:, t % 4, q, :], probs[:, t % 4, q, :], ACT.Exp,
                                         bias=neg_max[:, t, q:q + 1], scale=-1.0,
                                         accum_out=row_sum[:, t, q:q + 1]).then_inc(probs_ready, 1)

            def copy_turned(j, t):
                if t not in COPIED_BY_ACT:
                    return
                a = j - 1
                wait(act, pt_filled, STEPS * a + t + 1)
                wait(act, pv_done, QUADS * a + t // 4 - 1)
                nc.scalar.copy(probs_t[:, t % 8, :], pt_bank[t % 2][:]).then_inc(pt_by_act, 1)

            def copy_inverse(j, quad):
                unit = f"RT{quad}"
                wait_filled(act, j, unit)
                wait(act, attn_ready, QUADS * (j - 1) + quad - 1)
                nc.scalar.copy(inv_t[:, quad % 2, :], bank_of(unit)[:, 0:S]).then_inc(read[plan.bank(unit)], 1)

            def split_attn(j, quad):
                b, c = quad // KC, quad % KC
                if quad == 0:
                    if plan.has(j, 2):
                        wait_filled(act, j, "Wo1", back=1)
                wait(act, attn_ready, QUADS * (j - 1) + quad + 1)
                nc.scalar.copy(attn_hi[:, c, S * b:S * b + S], attn[:, quad % 2, :]).then_inc(attn_hi_ready, 1)

            def split_norm(j, which, k):
                unit = f"LN{which}T{k}"
                wait_filled(act, j, unit)
                if k == 0 and which == 1 and plan.has(j, 2):
                    wait_filled(act, j, "W1_7", back=1)
                if k == 0 and which == 2 and plan.has(j, 0):
                    wait_filled(act, j, "V1")
                nc.scalar.copy(norm_hi[:, k, :], bank_of(unit)[:]).then_inc(norm1_hi_ready if which == 1 else norm2_hi_ready, 1)

            def split_proj(j, m):
                unit = f"QK{m}"
                wait_filled(act, j, unit)
                if m % 2 == 0:
                    wait(act, stacked[m // 2], 16 * STACK_DMAS * j)
                nc.scalar.activation(proj_hi[:, m, :], bank_of(unit)[:], ACT.Identity,
                                     bias=qk_bias[:, 2 * (m % 2) + m // 2:2 * (m % 2) + m // 2 + 1],
                                     scale=1.0).then_inc(proj_hi_ready, 1)

            def copy_v(j, b):
                unit = f"V{b}"
                wait_filled(act, j, unit)
                wait(act, pv_done, QUADS * j)
                nc.scalar.copy(v_nat[:, b].rearrange("p t h -> p (t h)"),
                               bank_of(unit)[:]).then_inc(read[plan.bank(unit)], 1)

            def gelu(j, f):
                unit = f"W1_{f}"
                wait_filled(act, j, unit)
                wait(act, hid_hi_ready, FC * (j - 1) + f - 1)
                wait(act, hid_lo_ready, FC * (j - 1) + f - 1)
                nc.scalar.activation(hidden[:, f % 2, :], bank_of(unit)[:], ACT.Gelu, bias=b1_col[:, f:f + 1],
                                     scale=1.0).then_inc(read[plan.bank(unit)], 1)

            def body(j):
                now, before = plan.has(j, 0), plan.has(j, 1)
                if isinstance(j, int) and j == 0:
                    act.wait_ge(biases_ready, 1)
                if before:
                    for t in range(STEPS + 2):
                        if t < STEPS:
                            if t == 0 and isinstance(j, int) and j == 1:
                                act.wait_ge(weights_split, 6)
                                act.wait_ge(biases_ready, 3)
                            exps(j, t)
                        if t >= 2:
                            copy_turned(j, t - 2)
                        if t >= 7 and t % 4 == 3:
                            copy_inverse(j, (t - 7) // 4)
                        if t >= 9 and t % 4 == 1:
                            split_attn(j, (t - 9) // 4)
                if now:
                    split_norm(j, 1, 0)
                    split_norm(j, 1, 1)
                    split_proj(j, 0)
                    split_proj(j, 1)
                if before:
                    copy_inverse(j, 3)
                    split_attn(j, 3)
                if now:
                    split_proj(j, 2)
                    split_proj(j, 3)
                    copy_v(j, 0)
                    copy_v(j, 1)
                if before:
                    split_norm(j, 2, 0)
                    split_norm(j, 2, 1)
                    for f in range(FC):
                        gelu(j, f)

            run(act, body)

        @block.vector
        def _(dve):
            def split_weight(number, name, gain=None):
                hi, lo = split[name]
                dve.wait_ge(w_in[name], 16)
                if gain is None:
                    dve.wait_ge(hi_by_act, {"wo": 1, "w2": 2}[name])
                    nc.vector.tensor_tensor(lo[:], raw[name], hi[:].bitcast(F32), ALU.subtract).then_inc(weights_split, 1)
                    return
                for k in range(KC):
                    nc.vector.tensor_scalar(hi[:, k, :], raw[name][:, k, :], cols[:, gain + k:gain + k + 1], None,
                                            ALU.mult).then_inc(hi_by_dve, 1)
                for k in range(KC):
                    dve.wait_ge(hi_by_dve, KC * number + k + 1)
                    last = nc.vector.scalar_tensor_tensor(
                        out=lo[:, k, :], in0=raw[name][:, k, :], scalar=cols[:, gain + k:gain + k + 1],
                        in1=hi[:, k, :].bitcast(F32), op0=ALU.mult, op1=ALU.subtract)
                last.then_inc(weights_split, 1)

            def row_statistics(source, stats, step, moments, ready, first, count, group):
                for t in range(first, first + count):
                    nc.vector.bn_stats(stats[:, t, :], source[:, t, :]).then_inc(step, 1)
                for t in range(first, first + count):
                    wait(dve, step, TILES * group + t + 1)
                    carried(dve)
                    last = nc.vector.bn_aggr(moments[:, t, :], stats[:, t, :])
                last.then_inc(ready, 1)

            def ln1_statistics(j):
                wait(dve, x_ln1_in, 16 * (j + 2))
                row_statistics(norm1, stats1, stats1_step, moments1, moments1_ready, 0, TILES, j + 1)

            def ln1_normalise(j):
                wait(dve, rstd1_ready, j + 2)
                for t in range(TILES):
                    nc.vector.tensor_scalar(norm1[:, t, :], norm1[:, t, :], moments1[:, t, 0:1], rstd1[:, t:t + 1],
                                            ALU.subtract, ALU.mult).then_inc(norm1_ready, 1)

            def ln2_normalise(j):
                for t in range(TILES):
                    wait(dve, rstd2_ready, GB * (j - 1) + t // QT + 1)
                    nc.vector.tensor_scalar(norm2[:, t, :], x_mid[:, t, :], moments2[:, t, 0:1], rstd2[:, t:t + 1],
                                            ALU.subtract, ALU.mult).then_inc(norm2_ready, 1)

            def maxima(j, t):
                a, b = j - 1, t // HEADS
                if t == 0:
                    wait(dve, mask_ready, j)
                wait(dve, scores_ready, STEPS * a + t + 1)
                wait(dve, pt_filled, STEPS * a + t - 3)
                carried(dve)
                for q in range(QT):
                    nc.vector.tensor_tensor_reduce(probs[:, t % 4, q, :], score_bank[t % 2][:, S * q:S * q + S], mask_add[:, QT * b + q, :], -SCALE, HUGE, ALU.add,
                                                   ALU.min, neg_max[:, t, q:q + 1]).then_inc(max_ready, 1)

            def copy_turned(j, t):
                if t in COPIED_BY_ACT:
                    return
                a = j - 1
                wait(dve, pt_filled, STEPS * a + t + 1)
                wait(dve, pv_done, QUADS * a + t // 4 - 1)
                nc.vector.tensor_copy(probs_t[:, t % 8, :], pt_bank[t % 2][:]).then_inc(pt_by_dve, 1)

            def invert(j, quad):
                a = j - 1
                wait(dve, probs_ready, 2 * (STEPS * a + 4 * quad + 4))
                nc.vector.reciprocal(row_inv[:], row_sum[:, 4 * quad:4 * quad + 4, :]).then_inc(inv_ready, 1)
                if quad > 0:
                    wait_filled(dve, j, f"RT{quad - 1}")
                wait(dve, inv_ready, QUADS * a + quad + 1)
                nc.vector.tensor_copy(inv_wide[:], row_inv[:].rearrange("p g q -> p q g").unsqueeze(3)
                                      .broadcast_to([P, QT, 4, HD])).then_inc(wide_ready, 1)

            def normalise(j, quad):
                wait(dve, pv_done, QUADS * (j - 1) + quad + 1)
                wait_read(dve, j, f"RT{quad}")
                wait(dve, attn_hi_ready, QUADS * (j - 1) + quad - 1)
                nc.vector.tensor_tensor(attn[:, quad % 2, :], pv_bank[:, S * (quad % 2):S * (quad % 2) + S],
                                        inv_t[:, quad % 2, :], ALU.mult).then_inc(attn_ready, 1)

            def split_attn(j, quad):
                b, c = quad // KC, quad % KC
                wait(dve, attn_ready, QUADS * (j - 1) + quad + 1)
                wait(dve, attn_hi_ready, QUADS * (j - 1) + quad + 1)
                nc.vector.tensor_tensor(attn_lo[:, c, S * b:S * b + S], attn[:, quad % 2, :],
                                        attn_hi[:, c, S * b:S * b + S].bitcast(F32),
                                        ALU.subtract).then_inc(attn_lo_ready, 1)

            def split_norm(j, which, k):
                unit = f"LN{which}T{k}"
                ready, group = (norm1_hi_ready, j) if which == 1 else (norm2_hi_ready, j - 1)
                wait(dve, ready, KC * group + k + 1)
                nc.vector.tensor_tensor(norm_lo[:, k, :], bank_of(unit)[:], norm_hi[:, k, :].bitcast(F32),
                                        ALU.subtract).then_inc(read[plan.bank(unit)], 1)

            def split_proj(j, m):
                unit = f"QK{m}"
                wait(dve, proj_hi_ready, 4 * j + m + 1)
                nc.vector.scalar_tensor_tensor(
                    out=proj_lo[:, m, :], in0=bank_of(unit)[:],
                    scalar=qk_bias[:, 2 * (m % 2) + m // 2:2 * (m % 2) + m // 2 + 1],
                    in1=proj_hi[:, m, :].bitcast(F32), op0=ALU.add, op1=ALU.subtract).then_inc(read[plan.bank(unit)], 1)

            def add_attention(j, b):
                unit = f"Wo{b}"
                wait(dve, x_biased, j)
                wait_filled(dve, j, unit)
                tiles = x_mid[:, QT * b:QT * b + QT, :].rearrange("p t h -> p (t h)")
                nc.vector.tensor_tensor(tiles, bank_of(unit)[:], tiles, ALU.add).then_inc(read[plan.bank(unit)], 1)
                wait_read(dve, j, unit)
                row_statistics(x_mid, stats2, stats2_step, moments2, moments2_ready, QT * b, QT, j - 1)

            def add_mlp(j, half):
                unit = f"W2_{half}"
                wait(dve, result_seeded, j - 1)
                wait_filled(dve, j, unit)
                tiles = result[:, QT * half:QT * half + QT, :].rearrange("p t h -> p (t h)")
                nc.vector.tensor_tensor(tiles, bank_of(unit)[:], tiles, ALU.add).then_inc(read[plan.bank(unit)], 1)

            def round_hidden(j, f):
                wait_read(dve, j, f"W1_{f}")
                nc.vector.tensor_copy(hid_hi[:, f, :], hidden[:, f % 2, :]).then_inc(hid_hi_ready, 1)

            def body(j):
                now, before, two_before, after = (plan.has(j, back) for back in (0, 1, 2, -1))
                if isinstance(j, int) and j == 1:
                    dve.wait_ge(bias_mm, 2)
                    nc.vector.tensor_tensor(b1_col[:], score_bank[0][:, 0:FC], cols[:, B1:B1 + FC],
                                            ALU.add).then_inc(biases_ready, 1)
                    dve.wait_ge(bias_mm, 3)
                    nc.vector.tensor_tensor(bo_all[:], score_bank[1][:, 0:H], bo_all[:], ALU.add).then_inc(biases_ready, 1)
                for t in range(STEPS + 2):
                    if two_before and t == 9:
                        add_mlp(j, 0)
                    if two_before and t == 16:
                        add_mlp(j, 1)
                    if not before:
                        continue
                    if t < STEPS:
                        maxima(j, t)
                    if t >= 2:
                        copy_turned(j, t - 2)
                    if t >= 5 and t % 4 == 1:
                        invert(j, (t - 5) // 4)
                    if t >= 8 and t % 4 == 0:
                        normalise(j, (t - 8) // 4)
                    if t >= 9 and t % 4 == 1:
                        split_attn(j, (t - 9) // 4)
                if now:
                    split_norm(j, 1, 0)
                    split_norm(j, 1, 1)
                    split_proj(j, 0)
                    split_proj(j, 1)
                if before:
                    normalise(j, 3)
                    split_attn(j, 3)
                    add_attention(j, 0)
                if now:
                    split_proj(j, 2)
                if before:
                    add_attention(j, 1)
                if now:
                    split_proj(j, 3)
                if before:
                    ln2_normalise(j)
                    split_norm(j, 2, 0)
                    split_norm(j, 2, 1)
                    for f in range(FC // 2):
                        round_hidden(j, f)
                if after:
                    ln1_statistics(j)
                if before:
                    for f in range(FC // 2, FC):
                        round_hidden(j, f)
                if after:
                    ln1_normalise(j)
                if isinstance(j, int) and j == 0:
                    split_weight(3, "w1", G2)
                    split_weight(None, "wo")
                    split_weight(None, "w2")

            dve.wait_ge(consts_in, 16 * 3)
            split_weight(0, "wq", G1)
            split_weight(1, "wk", G1)
            split_weight(2, "wv", G1)
            dve.wait_ge(bias_mm, 1)
            nc.vector.tensor_tensor(bv_col[:], pv_bank[:, 4:4 + KC], cols[:, BV:BV + KC], ALU.add).then_inc(bv_ready, 1)
            nc.vector.tensor_tensor(qk_bias[:], pv_bank[:, 0:4], cols[:, BQ:BQ + 4], ALU.add).then_inc(biases_ready, 1)
            dve.wait_ge(bv_ready, 1)
            nc.vector.tensor_copy(inv_t[:, 0, :].rearrange("p (k m) -> p k m", k=KC),
                                  bv_col[:].unsqueeze(2).broadcast_to([P, KC, P])).then_inc(bv_spread, 1)
            run(dve, body, first=-1)

        @block.gpsimd
        def _(pool):
            nc.gpsimd.memset(neg_half[:], -0.5).then_inc(half_ready, 1)
            nc.gpsimd.memset(ident[:], 0.0).then_inc(ident_ready, 1)
            pool.wait_ge(ident_ready, 1)
            nc.gpsimd.affine_select(out=ident[:], in_=ident[:], compare_op=ALU.not_equal, fill=1.0, base=0,
                                    pattern=[[-1, P]], channel_multiplier=1).then_inc(ident_ready, 1)
            pool.wait_ge(half_ready, 1)

            def inverse_deviation(moments, var, var_ready, rstd, ready, first, count, number):
                tiles = slice(first, first + count)
                carried(pool)
                nc.gpsimd.tensor_scalar(var[:, tiles], moments[:, tiles, 1], LN_EPS, 1.0, ALU.add,
                                        ALU.mult).then_inc(var_ready, 1)
                wait(pool, var_ready, number)
                nc.gpsimd.tensor_tensor(rstd[:, tiles], var[:, tiles], neg_half[:, tiles], ALU.pow).then_inc(ready, 1)

            def body(j):
                now, before, after = (plan.has(j, back) for back in (0, 1, -1))
                if before:
                    if isinstance(j, int) and j == 1:
                        pool.wait_ge(biases_ready, 3)
                    wait(pool, x_mid_in, 16 * j)
                    nc.gpsimd.tensor_tensor(x_mid[:], x_mid[:], bo_all[:].unsqueeze(1).broadcast_to([P, TILES, H]),
                                            ALU.add).then_inc(x_biased, 1)
                if now:
                    wait(pool, adj_in, 16 * (j + 1))
                    wait(pool, max_ready, 2 * STEPS * j)
                    carried(pool)
                    nc.gpsimd.tensor_scalar(mask_add[:], adj_u8[:], -1.0, MASKED, ALU.add,
                                            ALU.mult).then_inc(mask_ready, 1)
                if before:
                    for b in range(GB):
                        wait(pool, moments2_ready, GB * (j - 1) + b + 1)
                        inverse_deviation(moments2, var2, var2_ready, rstd2, rstd2_ready, QT * b, QT,
                                          GB * (j - 1) + b + 1)
                    wait(pool, stored, 16 * GB * (j - 1))
                    nc.gpsimd.tensor_tensor(result[:], x_mid[:], b2_all[:].unsqueeze(1).broadcast_to([P, TILES, H]),
                                            ALU.add).then_inc(result_seeded, 1)
                for f in range(FC):
                    if before:
                        wait(pool, hid_hi_ready, FC * (j - 1) + f + 1)
                        nc.gpsimd.tensor_tensor(hid_lo[:, f, :], hidden[:, f % 2, :], hid_hi[:, f, :].bitcast(F32),
                                                ALU.subtract).then_inc(hid_lo_ready, 1)
                    if after and f == FC // 2:
                        wait(pool, moments1_ready, j + 2)
                        inverse_deviation(moments1, var1, var1_ready, rstd1, rstd1_ready, 0, TILES, j + 2)

            run(pool, body, first=-1)


def columns_of(*vectors):
    import numpy as np

    return np.ascontiguousarray(np.concatenate([v.reshape(-1, P).T for v in vectors], axis=1))


def kernel(x, adj, L0_gnn_ln1_g, L0_gnn_ln1_b, L0_gnn_ln2_g, L0_gnn_ln2_b, L0_gnn_Wq, L0_gnn_bq, L0_gnn_Wk,
           L0_gnn_bk, L0_gnn_Wv, L0_gnn_bv, L0_gnn_Wo, L0_gnn_bo, L0_gnn_W1, L0_gnn_b1, L0_gnn_W2, L0_gnn_b2):
    import numpy as np
    from concourse import bacc
    from concourse.bass_utils import run_bass_kernel_spmd

    columns = columns_of(*(np.asarray(v) for v in (
        L0_gnn_ln1_g, L0_gnn_ln1_b, L0_gnn_ln2_g, L0_gnn_ln2_b, L0_gnn_bq, L0_gnn_bk, L0_gnn_bv, L0_gnn_b1)))
    inputs = {
        "x": x, "adj": adj, "columns": columns,
        "bo_row": np.asarray(L0_gnn_bo), "b2_row": np.asarray(L0_gnn_b2),
        "wq": L0_gnn_Wq, "wk": L0_gnn_Wk, "wv": L0_gnn_Wv, "wo": L0_gnn_Wo, "w1": L0_gnn_W1, "w2": L0_gnn_W2,
    }
    nc = bacc.Bacc("TRN2", target_bir_lowering=False, num_devices=1)
    arrays, args = {}, []
    for name, a in inputs.items():
        a = np.ascontiguousarray(a)
        arrays[f"in_{name}"] = a
        args.append(nc.dram_tensor(f"in_{name}", a.shape, mybir.dt.from_np(a.dtype), kind="ExternalInput").ap())
    args.append(nc.dram_tensor("out", np.asarray(x).shape, F32, kind="ExternalOutput").ap())
    gnn_block(nc, *args)
    return run_bass_kernel_spmd(nc, [arrays], core_ids=[0]).results[0]["out"]
```

```python
from contextlib import ExitStack

import concourse.bass as bass
from concourse import mybir

ALU = mybir.AluOpType
ACT = mybir.ActivationFunctionType
AX = mybir.AxisListType
F32 = mybir.dt.float32
F32R = mybir.dt.float32r
U8 = mybir.dt.uint8

P = 128
HEADS = 8
LN_EPS = 1e-5
MASKED = 1e30
HUGE = 3e38

DENSE_BANK = {
    "W2_0": 0, "RT0": 1, "W2_1": 2, "RT1": 1, "RT2": 1, "LN1T0": 0, "LN1T1": 1, "RT3": 0, "QK0": 2,
    "QK1": 1, "Wo0": 0, "Wo1": 2, "QK2": 1, "QK3": 0, "V0": 2, "LN2T0": 1, "LN2T1": 0, "V1": 2,
    "W1_0": 1, "W1_1": 0, "W1_2": 2, "W1_3": 1, "W1_4": 0, "W1_5": 2, "W1_6": 1, "W1_7": 0,
}
DENSE_BANKS = 3
COPIED_BY_ACT = (0, 2, 5, 7, 9, 12, 14)
STEPS = 16


class Plan:

    def __init__(self, groups):
        self.groups = groups
        self.looped = (3, groups - 1)

    def has(self, j, back):
        return not isinstance(j, int) or 0 <= j - back < self.groups

    def units(self, j):
        def there(name):
            if name.startswith("W2"):
                return self.has(j, 2)
            if name[:2] in ("RT", "Wo", "W1") or name.startswith("LN2"):
                return self.has(j, 1)
            return self.has(j, 0)

        return [n for n in DENSE_BANK if there(n)]

    def bank(self, name):
        return DENSE_BANK[name]

    def uses(self, j, name, back=0):
        bank = self.bank(name)

        def in_iteration(k):
            return sum(self.bank(n) == bank for n in self.units(k))

        def before(k):
            return sum(in_iteration(i) for i in range(k))

        first = self.looped[0]
        units = self.units(j - back if isinstance(j, int) else first)
        here = sum(self.bank(n) == bank for n in units[: units.index(name) + 1])
        if isinstance(j, int):
            return before(j - back) + here
        each = in_iteration(first)
        return j * each + (before(first) + here - each * (first + back))


def wait(engine, semaphore, count):
    if isinstance(count, int) and count <= 0:
        return
    engine.wait_ge(semaphore, count)


def copied(step, by_act):
    return sum((s in COPIED_BY_ACT) == by_act for s in range(step + 1))


def gnn_block(nc, x, adj, columns, bo_row, b2_row, wq, wk, wv, wo, w1, w2, out):
    B, S, H = x.shape
    FF = w1.shape[1]
    HD = H // HEADS
    KC = H // P
    FC = FF // P
    GB = 2
    G = B // GB
    QT = S // P
    TOK = GB * S
    TILES = TOK // P
    QUADS = GB * KC
    assert (KC, FC, QT, HD, STEPS) == (2, 8, 2, 32, GB * HEADS)
    plan = Plan(G)
    SCALE = float(HD) ** -0.5
    STACK_DMAS = 4 * 4

    x_dram = x.rearrange("b (t p) h -> p (b t) h", p=P)
    out_dram = out.rearrange("b (t p) h -> p (b t) h", p=P)
    adj_dram = adj.rearrange("b (t p) k -> p (b t) k", p=P)

    with ExitStack() as ctx:
        def sb(name, shape, dt=F32):
            return ctx.enter_context(nc.sbuf_tensor(name, shape, dt))

        def psum(name):
            return ctx.enter_context(nc.psum_tensor(name, [P, 512], F32))

        def sem(name):
            return ctx.enter_context(nc.semaphore(name))

        split = {}
        for name, chunks, width in (("wq", KC, H), ("wk", KC, H), ("wv", KC, H), ("wo", KC, H),
                                    ("w1", KC, FF), ("w2", FC, H)):
            split[name] = (sb(f"{name}_hi", [P, chunks, width], F32R), sb(f"{name}_lo", [P, chunks, width], F32R))
        cols = sb("cols", [P, columns.shape[1]])
        qk_bias = sb("qk_bias", [P, 4])
        bv_col = sb("bv_col", [P, KC])
        b1_col = sb("b1_col", [P, FC])
        bo_all = sb("bo_all", [P, H])
        b2_all = sb("b2_all", [P, H])
        ident = sb("ident", [P, P])
        neg_half = sb("neg_half", [P, TILES])

        norm1 = sb("norm1", [P, TILES, H])
        norm1_hi = sb("norm1_hi", [P, KC, TOK], F32R)
        norm1_lo = sb("norm1_lo", [P, KC, TOK], F32R)
        proj = sb("proj", [P, KC, 4, TOK], F32R)
        stack = sb("stack", [P, 2, HEADS, TOK], F32R)
        v_nat = sb("v_nat", [P, GB, QT, H])
        adj_u8 = sb("adj_u8", [P, TILES, S], U8)
        mask_add = sb("mask_add", [P, TILES, S])
        neg_max = sb("neg_max", [P, STEPS, QT])
        row_sum = sb("row_sum", [P, STEPS, QT])
        row_inv = sb("row_inv", [P, 4, QT])
        inv_wide = sb("inv_wide", [P, QT, 4, HD])
        probs = sb("probs", [P, 4, QT, S])
        probs_t = sb("probs_t", [P, 8, 512])
        inv_t = sb("inv_t", [P, 2, S])
        attn = sb("attn", [P, 2, S])
        attn_hi = sb("attn_hi", [P, KC, TOK], F32R)
        attn_lo = sb("attn_lo", [P, KC, TOK], F32R)
        norm2_hi, norm2_lo = attn_hi, attn_lo
        x_mid = sb("x_mid", [P, TILES, H])
        norm2 = sb("norm2", [P, TILES, H])
        result = sb("result", [P, TILES, H])
        hidden = sb("hidden", [P, 2, TOK])
        hid_hi = sb("hid_hi", [P, FC, TOK], F32R)
        hid_lo = sb("hid_lo", [P, FC, TOK], F32R)
        stats1 = sb("stats1", [P, TILES, 6])
        stats2 = sb("stats2", [P, TILES, 6])
        moments1 = sb("moments1", [P, TILES, 2])
        moments2 = sb("moments2", [P, TILES, 2])
        var1 = sb("var1", [P, TILES])
        var2 = sb("var2", [P, TILES])
        rstd1 = sb("rstd1", [P, TILES])
        rstd2 = sb("rstd2", [P, TILES])

        raw = {
            "wq": probs[:, 0].rearrange("p a b -> p (a b)").rearrange("p (c n) -> p c n", c=KC),
            "wk": probs[:, 1].rearrange("p a b -> p (a b)").rearrange("p (c n) -> p c n", c=KC),
            "wv": probs[:, 2].rearrange("p a b -> p (a b)").rearrange("p (c n) -> p c n", c=KC),
            "wo": probs[:, 3].rearrange("p a b -> p (a b)").rearrange("p (c n) -> p c n", c=KC),
            "w1": probs_t[:, 0:4].rearrange("p a b -> p (a b)").rearrange("p (c n) -> p c n", c=KC),
            "w2": probs_t[:, 4:8].rearrange("p a b -> p (a b)").rearrange("p (c n) -> p c n", c=FC),
        }
        G1, BE1, G2, BE2, BQ, BK, BV, B1 = 0, 2, 4, 6, 8, 10, 12, 14

        score_bank = [psum(f"score_bank{i}") for i in range(2)]
        pt_bank = [psum(f"pt_bank{i}") for i in range(2)]
        pv_bank = psum("pv_bank")
        dense = [psum(f"dense{i}") for i in range(DENSE_BANKS)]

        consts_in = sem("consts_in")
        passed = sem("passed")
        w_in = {name: sem(f"{name}_in") for name in split}
        ident_ready, half_ready = sem("ident_ready"), sem("half_ready")
        bias_mm, biases_ready, bv_ready, bv_spread = (
            sem("bias_mm"), sem("biases_ready"), sem("bv_ready"), sem("bv_spread"))
        hi_by_dve, hi_by_act, weights_split = sem("hi_by_dve"), sem("hi_by_act"), sem("weights_split")
        x_ln1_in, x_mid_in, adj_in = sem("x_ln1_in"), sem("x_mid_in"), sem("adj_in")
        stats1_step, moments1_ready, var1_ready, rstd1_ready = (
            sem("stats1_step"), sem("moments1_ready"), sem("var1_ready"), sem("rstd1_ready"))
        stats2_step, moments2_ready, var2_ready, rstd2_ready = (
            sem("stats2_step"), sem("moments2_ready"), sem("var2_ready"), sem("rstd2_ready"))
        norm1_ready, norm2_ready = sem("norm1_ready"), sem("norm2_ready")
        norm1_hi_ready, norm2_hi_ready = sem("norm1_hi_ready"), sem("norm2_hi_ready")
        proj_hi_ready = sem("proj_hi_ready")
        stacked = [sem(f"stacked{c}") for c in range(KC)]
        mask_ready = sem("mask_ready")
        scores_ready, max_ready, probs_ready = sem("scores_ready"), sem("max_ready"), sem("probs_ready")
        pt_filled, pt_by_act, pt_by_dve = sem("pt_filled"), sem("pt_by_act"), sem("pt_by_dve")
        inv_ready, wide_ready = sem("inv_ready"), sem("wide_ready")
        pv_done, attn_ready, attn_hi_ready, attn_lo_ready = (
            sem("pv_done"), sem("attn_ready"), sem("attn_hi_ready"), sem("attn_lo_ready"))
        x_biased, result_seeded = sem("x_biased"), sem("result_seeded")
        hid_hi_ready, hid_lo_ready = sem("hid_hi_ready"), sem("hid_lo_ready")
        stored = sem("stored")
        filled = [sem(f"filled{i}") for i in range(DENSE_BANKS)]
        read = [sem(f"read{i}") for i in range(DENSE_BANKS)]

        def run(engine, body, first=0):
            lo, hi = plan.looped
            for j in range(first, lo):
                body(j)
            with engine.Fori(lo, hi) as j:
                body(j)
            for j in range(hi, G + 2):
                body(j)

        def carried(engine):
            engine.sem_inc(passed, 1)

        def wait_filled(engine, j, unit, back=0):
            wait(engine, filled[plan.bank(unit)], plan.uses(j, unit, back))

        def wait_free(engine, j, unit):
            wait(engine, read[plan.bank(unit)], plan.uses(j, unit) - 1)

        def wait_read(engine, j, unit, back=0):
            wait(engine, read[plan.bank(unit)], plan.uses(j, unit, back))

        def bank_of(unit):
            return dense[plan.bank(unit)]

        block = ctx.enter_context(nc.Block())

        @block.sync
        def _(sp):
            sp.dma_start(cols[:], columns).then_inc(consts_in, 16)
            sp.dma_start(bo_all[:], bo_row.partition_broadcast(P)).then_inc(consts_in, 16)
            sp.dma_start(b2_all[:], b2_row.partition_broadcast(P)).then_inc(consts_in, 16)
            sp.dma_start(norm1[:], x_dram[:, 0:TILES]).then_inc(x_ln1_in, 16)
            for name, w in (("wq", wq), ("wk", wk), ("wv", wv), ("wo", wo), ("w1", w1), ("w2", w2)):
                sp.dma_start(raw[name], w.rearrange("(c p) n -> p c n", p=P)).then_inc(w_in[name], 16)

            def body(j):
                if plan.has(j, 1):
                    wait(sp, norm2_ready, TILES * (j - 1))
                    carried(sp)
                    wait(sp, result_seeded, j - 1)
                    carried(sp)
                    sp.dma_start(x_mid[:], x_dram[:, bass.ds((j - 1) * TILES, TILES)]).then_inc(x_mid_in, 16)
                if plan.has(j, 0):
                    wait(sp, mask_ready, j)
                    carried(sp)
                    sp.dma_start(adj_u8[:], adj_dram[:, bass.ds(j * TILES, TILES)]).then_inc(adj_in, 16)
                if plan.has(j, 2):
                    for u in range(GB):
                        wait_read(sp, j, f"W2_{u}")
                        carried(sp)
                        sp.dma_start(out_dram[:, bass.ds((j - 2) * TILES + QT * u, QT)],
                                     result[:, QT * u:QT * u + QT]).then_inc(stored, 16)
                if plan.has(j, -1):
                    wait_filled(sp, j, "LN1T1")
                    carried(sp)
                    sp.dma_start(norm1[:], x_dram[:, bass.ds((j + 1) * TILES, TILES)]).then_inc(x_ln1_in, 16)
                if plan.has(j, 0):
                    wait(sp, scores_ready, STEPS * j)
                    carried(sp)
                    for c in range(KC):
                        wait_read(sp, j, f"QK{2 * c}")
                        carried(sp)
                        wait_read(sp, j, f"QK{2 * c + 1}")
                        carried(sp)
                        for r, parts in enumerate((slice(0, 3, 2), slice(0, 4, 3), slice(1, 3, 1), slice(1, 4, 2))):
                            for g in range(4):
                                sp.dma_start(stack[HD * r:HD * r + HD, :, 4 * c + g].bitcast(F32),
                                             proj[HD * g:HD * g + HD, c, parts].bitcast(F32)).then_inc(stacked[c], 16)

            run(sp, body)
            sp.wait_ge(stored, 16 * GB * G)

        @block.tensor
        def _(pe):
            def beta_products(bank, names, beta):
                column = 0
                for name in names:
                    pe.wait_ge(w_in[name], 16)
                    for m in range(split[name][0].shape[2] // P):
                        for k in range(KC):
                            last = pe.matmul(bank[:, column:column + 1], raw[name][:, k, P * m:P * m + P],
                                             cols[:, beta + k:beta + k + 1], start=(k == 0), stop=(k == KC - 1))
                        column += 1
                last.then_inc(bias_mm, 1)

            pe.wait_ge(consts_in, 16 * 3)
            beta_products(pv_bank, ("wq", "wk", "wv"), BE1)
            pe.wait_ge(ident_ready, 2)

            def three(bank, lhs, rhs, chunks, release=None):
                n = 0
                for c in range(chunks):
                    for a, b in ((0, 0), (0, 1), (1, 0)):
                        last = pe.matmul(bank, lhs(a, c), rhs(b, c), start=(n == 0), stop=(n == 3 * chunks - 1))
                        n += 1
                if release is not None:
                    last.then_inc(release, 1)

            ln1 = (norm1_hi, norm1_lo)
            ln2 = (norm2_hi, norm2_lo)
            att = (attn_hi, attn_lo)
            hid = (hid_hi, hid_lo)

            def scores(a, t):
                b, h = t // HEADS, t % HEADS
                if t in (0, 4):
                    wait(pe, stacked[t // 4], 16 * STACK_DMAS * (a + 1))
                wait(pe, max_ready, 2 * (STEPS * a + t - 1))
                for q in range(QT):
                    last = pe.matmul(score_bank[t % 2][:, S * q:S * q + S],
                                     stack[:, 0, h, S * b + P * q:S * b + P * q + P],
                                     stack[:, 1, h, S * b:S * b + S], start=True, stop=True)
                last.then_inc(scores_ready, 1)

            def turn(j, t):
                a = j - 1
                wait(pe, probs_ready, 2 * (STEPS * a + t + 1))
                before, turns = (t - 2, a) if t >= 2 else (t - 2 + STEPS, a - 1)
                if before in COPIED_BY_ACT:
                    wait(pe, pt_by_act, turns * copied(STEPS - 1, True) + copied(before, True))
                else:
                    wait(pe, pt_by_dve, turns * copied(STEPS - 1, False) + copied(before, False))
                for k in range(QT):
                    for q in range(QT):
                        last = pe.transpose(pt_bank[t % 2][:, S * k + P * q:S * k + P * q + P],
                                            probs[:, t % 4, q, P * k:P * k + P], ident[:])
                last.then_inc(pt_filled, 1)

            def values(j, quad):
                a, b, c = j - 1, quad // KC, quad % KC
                if quad == 0:
                    wait_read(pe, j, "V0", back=1)
                    wait_read(pe, j, "V1", back=1)
                last_step = 4 * quad + 3
                wait(pe, pt_by_act, a * copied(STEPS - 1, True) + copied(last_step, True))
                wait(pe, pt_by_dve, a * copied(STEPS - 1, False) + copied(last_step, False))
                wait(pe, attn_ready, QUADS * a + quad)
                for k in range(QT):
                    for g in range(4):
                        h = 4 * c + g
                        last = pe.matmul(pv_bank[HD * g:HD * g + HD, S * (quad % 2):S * (quad % 2) + S],
                                         v_nat[:, b, k, HD * h:HD * h + HD],
                                         probs_t[:, (4 * quad + g) % 8, S * k:S * k + S],
                                         start=(k == 0), stop=(k == QT - 1))
                last.then_inc(pv_done, 1)

            def turn_inverse(j, quad):
                unit = f"RT{quad}"
                wait(pe, wide_ready, QUADS * (j - 1) + quad + 1)
                wait_free(pe, j, unit)
                for q in range(QT):
                    last = pe.transpose(bank_of(unit)[:, P * q:P * q + P],
                                        inv_wide[:, q].rearrange("p g d -> p (g d)"), ident[:])
                last.then_inc(filled[plan.bank(unit)], 1)

            def mlp_out(j, half, piece, u):
                unit, tile = f"W2_{half}", QT * half + u
                if piece == 0 and u == 0:
                    wait_free(pe, j, unit)
                if half == 0 and u == 0:
                    wait(pe, hid_hi_ready, FC * (j - 2) + piece + 1)
                    wait(pe, hid_lo_ready, FC * (j - 2) + piece + 1)
                for n, (a, b) in enumerate(((0, 0), (0, 1), (1, 0))):
                    last = pe.matmul(bank_of(unit)[:, H * u:H * u + H], hid[a][:, piece, P * tile:P * tile + P],
                                     split["w2"][b][:, piece, :], start=(piece == 0 and u == 0 and n == 0),
                                     stop=(piece == FC - 1 and n == 2), skip_group_check=True)
                if piece == FC - 1 and u == QT - 1:
                    last.then_inc(filled[plan.bank(unit)], 1)

            def turn_norm(j, which, k):
                unit = f"LN{which}T{k}"
                source, ready, group = (norm1, norm1_ready, j) if which == 1 else (norm2, norm2_ready, j - 1)
                wait_free(pe, j, unit)
                for t in range(TILES):
                    if k == 0:
                        wait(pe, ready, TILES * group + t + 1)
                    last = pe.transpose(bank_of(unit)[:, P * t:P * t + P], source[:, t, P * k:P * k + P], ident[:])
                last.then_inc(filled[plan.bank(unit)], 1)

            def project(j, m):
                unit, w = f"QK{m}", split["wk" if m % 2 else "wq"]
                if m == 0:
                    wait_read(pe, j, "LN1T0")
                    wait_read(pe, j, "LN1T1")
                wait_free(pe, j, unit)
                c = m // 2
                three(bank_of(unit)[:], lambda a, k: w[a][:, k, P * c:P * c + P], lambda b, k: ln1[b][:, k, :],
                      KC, filled[plan.bank(unit)])

            def project_v(j, b):
                unit = f"V{b}"
                wait_free(pe, j, unit)
                for t in range(QT):
                    tile = QT * b + t
                    three(bank_of(unit)[:, H * t:H * t + H], lambda a, k: ln1[a][:, k, P * tile:P * tile + P],
                          lambda c, k: split["wv"][c][:, k, :], KC, filled[plan.bank(unit)] if t == QT - 1 else None)

            def project_out(j, b):
                unit = f"Wo{b}"
                done = QUADS * (j - 1) + KC * (b + 1)
                wait(pe, attn_hi_ready, done)
                wait(pe, attn_lo_ready, done)
                wait_free(pe, j, unit)
                for t in range(QT):
                    tile = QT * b + t
                    three(bank_of(unit)[:, H * t:H * t + H], lambda a, k: att[a][:, k, P * tile:P * tile + P],
                          lambda c, k: split["wo"][c][:, k, :], KC, filled[plan.bank(unit)] if t == QT - 1 else None)

            def mlp_in(j, f):
                unit, w = f"W1_{f}", split["w1"]
                if f == 0:
                    wait_read(pe, j, "LN2T0")
                    wait_read(pe, j, "LN2T1")
                wait_free(pe, j, unit)
                three(bank_of(unit)[:], lambda a, k: w[a][:, k, P * f:P * f + P], lambda b, k: ln2[b][:, k, :],
                      KC, filled[plan.bank(unit)])

            def body(j):
                now, before, two_before = plan.has(j, 0), plan.has(j, 1), plan.has(j, 2)
                if isinstance(j, int) and j == 0:
                    pe.wait_ge(weights_split, 3)
                if isinstance(j, int) and j == 1:
                    beta_products(pt_bank[0], ("w1",), BE2)
                    pe.wait_ge(w_in["wo"], 16)
                    pe.wait_ge(bv_spread, 1)
                    for k in range(KC):
                        last = pe.matmul(pt_bank[1][:, 0:H], inv_t[:, 0, P * k:P * k + P], raw["wo"][:, k, :],
                                         start=(k == 0), stop=(k == KC - 1))
                    last.then_inc(bias_mm, 1)
                    pe.wait_ge(biases_ready, 3)
                    pe.wait_ge(weights_split, 6)
                for t in range(STEPS):
                    if before and t + 2 < STEPS:
                        scores(j - 1, t + 2)
                    if two_before:
                        mlp_out(j, t // 8, t % 8, 0)
                    if before and t >= 1:
                        turn(j, t - 1)
                    if now and t == 14:
                        turn_norm(j, 1, 0)
                    if two_before:
                        mlp_out(j, t // 8, t % 8, 1)
                    if before and t % 4 == 2 and t > 2:
                        turn_inverse(j, (t - 6) // 4)
                        values(j, (t - 6) // 4)
                if now:
                    turn_norm(j, 1, 1)
                if before:
                    turn(j, 15)
                    turn_inverse(j, 3)
                if now:
                    project(j, 0)
                if before:
                    values(j, 3)
                if now:
                    project(j, 1)
                if before:
                    project_out(j, 0)
                    project_out(j, 1)
                if now:
                    project(j, 2)
                    project(j, 3)
                    project_v(j, 0)
                if before:
                    turn_norm(j, 2, 0)
                    turn_norm(j, 2, 1)
                if now:
                    project_v(j, 1)
                for f in range(FC):
                    if now and f >= FC - 2:
                        scores(j, f - (FC - 2))
                    if before:
                        mlp_in(j, f)

            run(pe, body)

        @block.scalar
        def _(act):
            for name in ("wo", "w2"):
                act.wait_ge(w_in[name], 16)
                nc.scalar.copy(split[name][0][:], raw[name]).then_inc(hi_by_act, 1)

            def exps(j, t):
                a = j - 1
                for q in range(QT):
                    wait(act, max_ready, 2 * (STEPS * a + t) + q + 1)
                    nc.scalar.activation(probs[:, t % 4, q, :], probs[:, t % 4, q, :], ACT.Exp,
                                         bias=neg_max[:, t, q:q + 1], scale=-1.0,
                                         accum_out=row_sum[:, t, q:q + 1]).then_inc(probs_ready, 1)

            def copy_turned(j, t):
                if t not in COPIED_BY_ACT:
                    return
                a = j - 1
                wait(act, pt_filled, STEPS * a + t + 1)
                wait(act, pv_done, QUADS * a + t // 4 - 1)
                nc.scalar.copy(probs_t[:, t % 8, :], pt_bank[t % 2][:]).then_inc(pt_by_act, 1)

            def copy_inverse(j, quad):
                unit = f"RT{quad}"
                wait_filled(act, j, unit)
                wait(act, attn_ready, QUADS * (j - 1) + quad - 1)
                nc.scalar.copy(inv_t[:, quad % 2, :], bank_of(unit)[:, 0:S]).then_inc(read[plan.bank(unit)], 1)

            def split_attn(j, quad):
                b, c = quad // KC, quad % KC
                if quad == 0 and plan.has(j, 2):
                    wait_filled(act, j, "W1_7", back=1)
                wait(act, attn_ready, QUADS * (j - 1) + quad + 1)
                nc.scalar.copy(attn_hi[:, c, S * b:S * b + S], attn[:, quad % 2, :]).then_inc(attn_hi_ready, 1)

            def split_norm(j, which, k):
                unit = f"LN{which}T{k}"
                wait_filled(act, j, unit)
                hi, ready = (norm1_hi, norm1_hi_ready) if which == 1 else (norm2_hi, norm2_hi_ready)
                if which == 2 and k == 0:
                    wait_filled(act, j, "Wo1")
                nc.scalar.copy(hi[:, k, :], bank_of(unit)[:]).then_inc(ready, 1)

            def split_proj(j, m):
                unit = f"QK{m}"
                wait_filled(act, j, unit)
                if m % 2 == 0:
                    wait(act, stacked[m // 2], 16 * STACK_DMAS * j)
                nc.scalar.activation(proj[:, m // 2, 2 * (m % 2), :], bank_of(unit)[:], ACT.Identity,
                                     bias=qk_bias[:, 2 * (m % 2) + m // 2:2 * (m % 2) + m // 2 + 1],
                                     scale=1.0).then_inc(proj_hi_ready, 1)

            def copy_v(j, b):
                unit = f"V{b}"
                wait_filled(act, j, unit)
                wait(act, pv_done, QUADS * j)
                nc.scalar.copy(v_nat[:, b].rearrange("p t h -> p (t h)"),
                               bank_of(unit)[:]).then_inc(read[plan.bank(unit)], 1)

            def gelu(j, f):
                unit = f"W1_{f}"
                wait_filled(act, j, unit)
                wait(act, hid_hi_ready, FC * (j - 1) + f - 1)
                wait(act, hid_lo_ready, FC * (j - 1) + f - 1)
                nc.scalar.activation(hidden[:, f % 2, :], bank_of(unit)[:], ACT.Gelu, bias=b1_col[:, f:f + 1],
                                     scale=1.0).then_inc(read[plan.bank(unit)], 1)

            def body(j):
                now, before = plan.has(j, 0), plan.has(j, 1)
                if isinstance(j, int) and j == 0:
                    act.wait_ge(biases_ready, 1)
                for t in range(STEPS + 1):
                    if before:
                        if t == 0 and isinstance(j, int) and j == 1:
                            act.wait_ge(biases_ready, 3)
                        if t < STEPS:
                            exps(j, t)
                        if t % 4 == 0 and t >= 8:
                            split_attn(j, (t - 8) // 4)
                        if t >= 1:
                            copy_turned(j, t - 1)
                        if t % 4 == 2 and t > 2:
                            copy_inverse(j, (t - 6) // 4)
                    if now and t == 15:
                        split_norm(j, 1, 0)
                if now:
                    split_norm(j, 1, 1)
                if before:
                    copy_inverse(j, 3)
                if now:
                    split_proj(j, 0)
                if before:
                    split_attn(j, 3)
                if now:
                    split_proj(j, 1)
                    split_proj(j, 2)
                    split_proj(j, 3)
                    copy_v(j, 0)
                if before:
                    split_norm(j, 2, 0)
                    split_norm(j, 2, 1)
                if now:
                    copy_v(j, 1)
                if before:
                    for f in range(FC):
                        gelu(j, f)

            run(act, body)

        @block.vector
        def _(dve):
            def split_weight(number, name, gain=None):
                hi, lo = split[name]
                dve.wait_ge(w_in[name], 16)
                if gain is None:
                    dve.wait_ge(hi_by_act, {"wo": 1, "w2": 2}[name])
                    nc.vector.tensor_tensor(lo[:], raw[name], hi[:].bitcast(F32), ALU.subtract).then_inc(weights_split, 1)
                    return
                for k in range(KC):
                    nc.vector.tensor_scalar(hi[:, k, :], raw[name][:, k, :], cols[:, gain + k:gain + k + 1], None,
                                            ALU.mult).then_inc(hi_by_dve, 1)
                for k in range(KC):
                    dve.wait_ge(hi_by_dve, KC * number + k + 1)
                    last = nc.vector.scalar_tensor_tensor(
                        out=lo[:, k, :], in0=raw[name][:, k, :], scalar=cols[:, gain + k:gain + k + 1],
                        in1=hi[:, k, :].bitcast(F32), op0=ALU.mult, op1=ALU.subtract)
                last.then_inc(weights_split, 1)

            def row_statistics(source, stats, step, moments, ready, first, count, group):
                for t in range(first, first + count):
                    nc.vector.bn_stats(stats[:, t, :], source[:, t, :]).then_inc(step, 1)
                for t in range(first, first + count):
                    wait(dve, step, TILES * group + t + 1)
                    carried(dve)
                    last = nc.vector.bn_aggr(moments[:, t, :], stats[:, t, :])
                last.then_inc(ready, 1)

            def ln1_statistics(j):
                wait(dve, x_ln1_in, 16 * (j + 2))
                row_statistics(norm1, stats1, stats1_step, moments1, moments1_ready, 0, TILES, j + 1)

            def ln1_normalise(j):
                wait(dve, rstd1_ready, j + 2)
                for t in range(TILES):
                    nc.vector.tensor_scalar(norm1[:, t, :], norm1[:, t, :], moments1[:, t, 0:1], rstd1[:, t:t + 1],
                                            ALU.subtract, ALU.mult).then_inc(norm1_ready, 1)

            def ln2_normalise(j, b):
                for t in range(QT * b, QT * b + QT):
                    wait(dve, rstd2_ready, GB * (j - 1) + t // QT + 1)
                    nc.vector.tensor_scalar(norm2[:, t, :], x_mid[:, t, :], moments2[:, t, 0:1], rstd2[:, t:t + 1],
                                            ALU.subtract, ALU.mult).then_inc(norm2_ready, 1)

            def maxima(a, t):
                b = t // HEADS
                if t == 0:
                    wait(dve, mask_ready, a + 1)
                wait(dve, scores_ready, STEPS * a + t + 1)
                wait(dve, pt_filled, STEPS * a + t - 3)
                carried(dve)
                for q in range(QT):
                    nc.vector.tensor_tensor_reduce(probs[:, t % 4, q, :], score_bank[t % 2][:, S * q:S * q + S], mask_add[:, QT * b + q, :], -SCALE, HUGE, ALU.add,
                                                   ALU.min, neg_max[:, t, q:q + 1]).then_inc(max_ready, 1)

            def copy_turned(j, t):
                if t in COPIED_BY_ACT:
                    return
                a = j - 1
                wait(dve, pt_filled, STEPS * a + t + 1)
                wait(dve, pv_done, QUADS * a + t // 4 - 1)
                nc.vector.tensor_copy(probs_t[:, t % 8, :], pt_bank[t % 2][:]).then_inc(pt_by_dve, 1)

            def invert(j, quad):
                a = j - 1
                wait(dve, probs_ready, 2 * (STEPS * a + 4 * quad + 4))
                nc.vector.reciprocal(row_inv[:], row_sum[:, 4 * quad:4 * quad + 4, :]).then_inc(inv_ready, 1)
                if quad > 0:
                    wait_filled(dve, j, f"RT{quad - 1}")
                wait(dve, inv_ready, QUADS * a + quad + 1)
                nc.vector.tensor_copy(inv_wide[:], row_inv[:].rearrange("p g q -> p q g").unsqueeze(3)
                                      .broadcast_to([P, QT, 4, HD])).then_inc(wide_ready, 1)

            def normalise(j, quad):
                wait(dve, pv_done, QUADS * (j - 1) + quad + 1)
                wait_read(dve, j, f"RT{quad}")
                wait(dve, attn_hi_ready, QUADS * (j - 1) + quad - 1)
                nc.vector.tensor_tensor(attn[:, quad % 2, :], pv_bank[:, S * (quad % 2):S * (quad % 2) + S],
                                        inv_t[:, quad % 2, :], ALU.mult).then_inc(attn_ready, 1)

            def split_attn(j, quad):
                b, c = quad // KC, quad % KC
                wait(dve, attn_ready, QUADS * (j - 1) + quad + 1)
                wait(dve, attn_hi_ready, QUADS * (j - 1) + quad + 1)
                nc.vector.tensor_tensor(attn_lo[:, c, S * b:S * b + S], attn[:, quad % 2, :],
                                        attn_hi[:, c, S * b:S * b + S].bitcast(F32),
                                        ALU.subtract).then_inc(attn_lo_ready, 1)

            def split_norm(j, which, k):
                unit = f"LN{which}T{k}"
                hi, lo, ready, group = ((norm1_hi, norm1_lo, norm1_hi_ready, j) if which == 1 else
                                        (norm2_hi, norm2_lo, norm2_hi_ready, j - 1))
                wait(dve, ready, KC * group + k + 1)
                nc.vector.tensor_tensor(lo[:, k, :], bank_of(unit)[:], hi[:, k, :].bitcast(F32),
                                        ALU.subtract).then_inc(read[plan.bank(unit)], 1)

            def split_proj(j, m):
                unit = f"QK{m}"
                wait(dve, proj_hi_ready, 4 * j + m + 1)
                nc.vector.scalar_tensor_tensor(
                    out=proj[:, m // 2, 2 * (m % 2) + 1, :], in0=bank_of(unit)[:],
                    scalar=qk_bias[:, 2 * (m % 2) + m // 2:2 * (m % 2) + m // 2 + 1],
                    in1=proj[:, m // 2, 2 * (m % 2), :].bitcast(F32), op0=ALU.add, op1=ALU.subtract).then_inc(read[plan.bank(unit)], 1)

            def add_attention(j, b):
                unit = f"Wo{b}"
                wait(dve, x_biased, j)
                wait_filled(dve, j, unit)
                tiles = x_mid[:, QT * b:QT * b + QT, :].rearrange("p t h -> p (t h)")
                nc.vector.tensor_tensor(tiles, bank_of(unit)[:], tiles, ALU.add).then_inc(read[plan.bank(unit)], 1)
                wait_read(dve, j, unit)
                row_statistics(x_mid, stats2, stats2_step, moments2, moments2_ready, QT * b, QT, j - 1)

            def add_mlp(j, half):
                unit = f"W2_{half}"
                wait(dve, result_seeded, j - 1)
                wait_filled(dve, j, unit)
                tiles = result[:, QT * half:QT * half + QT, :].rearrange("p t h -> p (t h)")
                nc.vector.tensor_tensor(tiles, bank_of(unit)[:], tiles, ALU.add).then_inc(read[plan.bank(unit)], 1)

            def round_hidden(j, f):
                wait_read(dve, j, f"W1_{f}")
                nc.vector.tensor_copy(hid_hi[:, f, :], hidden[:, f % 2, :]).then_inc(hid_hi_ready, 1)

            def body(j):
                now, before, two_before, after = (plan.has(j, back) for back in (0, 1, 2, -1))
                if isinstance(j, int) and j == 1:
                    dve.wait_ge(bias_mm, 2)
                    nc.vector.tensor_tensor(b1_col[:], pt_bank[0][:, 0:FC], cols[:, B1:B1 + FC],
                                            ALU.add).then_inc(biases_ready, 1)
                    dve.wait_ge(bias_mm, 3)
                    nc.vector.tensor_tensor(bo_all[:], pt_bank[1][:, 0:H], bo_all[:], ALU.add).then_inc(biases_ready, 1)
                for t in range(STEPS + 1):
                    if two_before and t == 9:
                        add_mlp(j, 0)
                    if two_before and t == 16:
                        add_mlp(j, 1)
                    if before:
                        if t + 2 < STEPS:
                            maxima(j - 1, t + 2)
                        if t >= 1:
                            copy_turned(j, t - 1)
                        if t % 4 == 0 and t > 0:
                            invert(j, (t - 4) // 4)
                        if t % 4 == 3 and t > 3:
                            normalise(j, (t - 7) // 4)
                        if t % 4 == 0 and t >= 8:
                            split_attn(j, (t - 8) // 4)
                    if now and t == 16:
                        split_norm(j, 1, 0)
                if now:
                    split_norm(j, 1, 1)
                    split_proj(j, 0)
                if before:
                    normalise(j, 3)
                    split_attn(j, 3)
                if now:
                    split_proj(j, 1)
                if before:
                    add_attention(j, 0)
                    add_attention(j, 1)
                if now:
                    split_proj(j, 2)
                if before:
                    ln2_normalise(j, 0)
                if now:
                    split_proj(j, 3)
                if before:
                    ln2_normalise(j, 1)
                    split_norm(j, 2, 0)
                    split_norm(j, 2, 1)
                for f in range(FC):
                    if before:
                        round_hidden(j, f)
                    if after and f == 2:
                        ln1_statistics(j)
                    if after and f == 5:
                        ln1_normalise(j)
                    if now and f >= FC - 3 and f < FC - 1:
                        maxima(j, f - (FC - 3))
                if isinstance(j, int) and j == 0:
                    split_weight(3, "w1", G2)
                    split_weight(None, "wo")
                    split_weight(None, "w2")

            dve.wait_ge(consts_in, 16 * 3)
            split_weight(0, "wq", G1)
            split_weight(1, "wk", G1)
            split_weight(2, "wv", G1)
            dve.wait_ge(bias_mm, 1)
            nc.vector.tensor_tensor(bv_col[:], pv_bank[:, 4:4 + KC], cols[:, BV:BV + KC], ALU.add).then_inc(bv_ready, 1)
            nc.vector.tensor_tensor(qk_bias[:], pv_bank[:, 0:4], cols[:, BQ:BQ + 4], ALU.add).then_inc(biases_ready, 1)
            dve.wait_ge(bv_ready, 1)
            nc.vector.tensor_copy(inv_t[:, 0, :].rearrange("p (k m) -> p k m", k=KC),
                                  bv_col[:].unsqueeze(2).broadcast_to([P, KC, P])).then_inc(bv_spread, 1)
            run(dve, body, first=-1)

        @block.gpsimd
        def _(pool):
            nc.gpsimd.memset(neg_half[:], -0.5).then_inc(half_ready, 1)
            nc.gpsimd.memset(ident[:], 0.0).then_inc(ident_ready, 1)
            pool.wait_ge(ident_ready, 1)
            nc.gpsimd.affine_select(out=ident[:], in_=ident[:], compare_op=ALU.not_equal, fill=1.0, base=0,
                                    pattern=[[-1, P]], channel_multiplier=1).then_inc(ident_ready, 1)
            pool.wait_ge(half_ready, 1)

            def inverse_deviation(moments, var, var_ready, rstd, ready, first, count, number):
                tiles = slice(first, first + count)
                carried(pool)
                nc.gpsimd.tensor_scalar(var[:, tiles], moments[:, tiles, 1], LN_EPS, 1.0, ALU.add,
                                        ALU.mult).then_inc(var_ready, 1)
                wait(pool, var_ready, number)
                nc.gpsimd.tensor_tensor(rstd[:, tiles], var[:, tiles], neg_half[:, tiles], ALU.pow).then_inc(ready, 1)

            def body(j):
                now, before, two_before, after = (plan.has(j, back) for back in (0, 1, 2, -1))
                if two_before:
                    wait(pool, stored, 16 * GB * (j - 2))
                    nc.gpsimd.tensor_tensor(result[:], x_mid[:], b2_all[:].unsqueeze(1).broadcast_to([P, TILES, H]),
                                            ALU.add).then_inc(result_seeded, 1)
                if before:
                    if isinstance(j, int) and j == 1:
                        pool.wait_ge(biases_ready, 3)
                    wait(pool, x_mid_in, 16 * j)
                    nc.gpsimd.tensor_tensor(x_mid[:], x_mid[:], bo_all[:].unsqueeze(1).broadcast_to([P, TILES, H]),
                                            ALU.add).then_inc(x_biased, 1)
                if now:
                    wait(pool, adj_in, 16 * (j + 1))
                    wait(pool, max_ready, 2 * STEPS * j)
                    carried(pool)
                    nc.gpsimd.tensor_scalar(mask_add[:], adj_u8[:], -1.0, MASKED, ALU.add,
                                            ALU.mult).then_inc(mask_ready, 1)
                if before:
                    for b in range(GB):
                        wait(pool, moments2_ready, GB * (j - 1) + b + 1)
                        inverse_deviation(moments2, var2, var2_ready, rstd2, rstd2_ready, QT * b, QT,
                                          GB * (j - 1) + b + 1)
                for f in range(FC):
                    if before:
                        wait(pool, hid_hi_ready, FC * (j - 1) + f + 1)
                        nc.gpsimd.tensor_tensor(hid_lo[:, f, :], hidden[:, f % 2, :], hid_hi[:, f, :].bitcast(F32),
                                                ALU.subtract).then_inc(hid_lo_ready, 1)
                    if after and f == 3:
                        wait(pool, moments1_ready, j + 2)
                        inverse_deviation(moments1, var1, var1_ready, rstd1, rstd1_ready, 0, TILES, j + 2)

            run(pool, body, first=-1)


def columns_of(*vectors):
    import numpy as np

    return np.ascontiguousarray(np.concatenate([v.reshape(-1, P).T for v in vectors], axis=1))


def kernel(x, adj, L0_gnn_ln1_g, L0_gnn_ln1_b, L0_gnn_ln2_g, L0_gnn_ln2_b, L0_gnn_Wq, L0_gnn_bq, L0_gnn_Wk,
           L0_gnn_bk, L0_gnn_Wv, L0_gnn_bv, L0_gnn_Wo, L0_gnn_bo, L0_gnn_W1, L0_gnn_b1, L0_gnn_W2, L0_gnn_b2):
    import numpy as np
    from concourse import bacc
    from concourse.bass_utils import run_bass_kernel_spmd

    columns = columns_of(*(np.asarray(v) for v in (
        L0_gnn_ln1_g, L0_gnn_ln1_b, L0_gnn_ln2_g, L0_gnn_ln2_b, L0_gnn_bq, L0_gnn_bk, L0_gnn_bv, L0_gnn_b1)))
    inputs = {
        "x": x, "adj": adj, "columns": columns,
        "bo_row": np.asarray(L0_gnn_bo), "b2_row": np.asarray(L0_gnn_b2),
        "wq": L0_gnn_Wq, "wk": L0_gnn_Wk, "wv": L0_gnn_Wv, "wo": L0_gnn_Wo, "w1": L0_gnn_W1, "w2": L0_gnn_W2,
    }
    nc = bacc.Bacc("TRN2", target_bir_lowering=False, num_devices=1)
    arrays, args = {}, []
    for name, a in inputs.items():
        a = np.ascontiguousarray(a)
        arrays[f"in_{name}"] = a
        args.append(nc.dram_tensor(f"in_{name}", a.shape, mybir.dt.from_np(a.dtype), kind="ExternalInput").ap())
    args.append(nc.dram_tensor("out", np.asarray(x).shape, F32, kind="ExternalOutput").ap())
    gnn_block(nc, *args)
    return run_bass_kernel_spmd(nc, [arrays], core_ids=[0]).results[0]["out"]
```

```python
from contextlib import ExitStack

import concourse.bass as bass
from concourse import mybir

ALU = mybir.AluOpType
ACT = mybir.ActivationFunctionType
F32 = mybir.dt.float32
F32R = mybir.dt.float32r
U8 = mybir.dt.uint8

P = 128
HEADS = 8
LN_EPS = 1e-5
MASKED = 1e30
HUGE = 3e38

DENSE_BANK = {
    "W2_0": 1, "W2_1": 2, "RT0": 0, "LN1T0": 1, "RT1": 0, "LN1T1": 1, "RT2": 0, "QK0": 1, "QK1": 2, "RT3": 0,
    "Wo0": 1, "QK2": 0, "Wo1": 2, "V0": 1, "V1": 2, "LN2T0": 1, "LN2T1": 2, "QK3": 0,
    "W1_0": 1, "W1_1": 2, "W1_2": 0, "W1_3": 1, "W1_4": 2, "W1_5": 0, "W1_6": 2, "W1_7": 0,
}
DENSE_BANKS = 3
COPIED_BY_ACT = (0, 2, 5, 7, 9, 11, 13, 15)
STEPS = 16
MLP_UNITS = (4, 4, 2, 2, 2, 2, 2, 1, 2, 2, 2, 1, 2, 1, 2, 1)


class Plan:

    def __init__(self, groups):
        self.groups = groups
        self.looped = (3, groups - 1)

    def has(self, j, back):
        return not isinstance(j, int) or 0 <= j - back < self.groups

    def units(self, j):
        def there(name):
            if name.startswith("W2"):
                return self.has(j, 2)
            if name[:2] in ("RT", "Wo", "W1") or name.startswith("LN2"):
                return self.has(j, 1)
            return self.has(j, 0)

        return [n for n in DENSE_BANK if there(n)]

    def bank(self, name):
        return DENSE_BANK[name]

    def uses(self, j, name, back=0):
        bank = self.bank(name)

        def in_iteration(k):
            return sum(self.bank(n) == bank for n in self.units(k))

        def before(k):
            return sum(in_iteration(i) for i in range(k))

        first = self.looped[0]
        units = self.units(j - back if isinstance(j, int) else first)
        here = sum(self.bank(n) == bank for n in units[: units.index(name) + 1])
        if isinstance(j, int):
            return before(j - back) + here
        each = in_iteration(first)
        return j * each + (before(first) + here - each * (first + back))


def wait(engine, semaphore, count):
    if isinstance(count, int) and count <= 0:
        return
    engine.wait_ge(semaphore, count)


def copied(step, by_act):
    return sum((s in COPIED_BY_ACT) == by_act for s in range(step + 1))


def gnn_block(nc, x, adj, columns, bo_row, b2_row, wq, wk, wv, wo, w1, w2, out):
    B, S, H = x.shape
    FF = w1.shape[1]
    HD = H // HEADS
    KC = H // P
    FC = FF // P
    GB = 2
    G = B // GB
    QT = S // P
    TOK = GB * S
    TILES = TOK // P
    QUADS = GB * KC
    assert (KC, FC, QT, HD, STEPS) == (2, 8, 2, 32, GB * HEADS)
    plan = Plan(G)
    SCALE = float(HD) ** -0.5
    STACK_DMAS = 2 * 4

    x_dram = x.rearrange("b (t p) h -> p (b t) h", p=P)
    out_dram = out.rearrange("b (t p) h -> p (b t) h", p=P)
    adj_dram = adj.rearrange("b (t p) k -> p (b t) k", p=P)

    with ExitStack() as ctx:
        def sb(name, shape, dt=F32):
            return ctx.enter_context(nc.sbuf_tensor(name, shape, dt))

        def psum(name):
            return ctx.enter_context(nc.psum_tensor(name, [P, 512], F32))

        def sem(name):
            return ctx.enter_context(nc.semaphore(name))

        split = {}
        for name, chunks, width in (("wq", KC, H), ("wk", KC, H), ("wv", KC, H), ("wo", KC, H),
                                    ("w1", KC, FF), ("w2", FC, H)):
            split[name] = (sb(f"{name}_hi", [P, chunks, width], F32R), sb(f"{name}_lo", [P, chunks, width], F32R))
        cols = sb("cols", [P, columns.shape[1]])
        qk_bias = sb("qk_bias", [P, 4])
        bv_col = sb("bv_col", [P, KC])
        b1_col = sb("b1_col", [P, FC])
        bo_all = sb("bo_all", [P, H])
        b2_all = sb("b2_all", [P, H])
        ident = sb("ident", [P, P])
        neg_half = sb("neg_half", [P, TILES])

        norm1 = sb("norm1", [P, TILES, H])
        norm1_hi = sb("norm1_hi", [P, KC, TOK], F32R)
        norm1_lo = sb("norm1_lo", [P, KC, TOK], F32R)
        proj = sb("proj", [P, KC, 4, TOK], F32R)
        stack = sb("stack", [P, 2, HEADS, TOK], F32R)
        v_nat = sb("v_nat", [P, GB, QT, H])
        adj_u8 = sb("adj_u8", [P, TILES, S], U8)
        mask_add = sb("mask_add", [P, TILES, S])
        neg_max = sb("neg_max", [P, STEPS, QT])
        row_sum = sb("row_sum", [P, STEPS, QT])
        row_inv = sb("row_inv", [P, 4, QT])
        inv_wide = sb("inv_wide", [P, QT, 4, HD])
        probs = sb("probs", [P, 4, QT, S])
        probs_t = sb("probs_t", [P, 8, 512])
        inv_t = sb("inv_t", [P, 2, S])
        attn = sb("attn", [P, 2, S])
        attn_hi = sb("attn_hi", [P, KC, TOK], F32R)
        attn_lo = sb("attn_lo", [P, KC, TOK], F32R)
        norm2_hi, norm2_lo = attn_hi, attn_lo
        x_mid = sb("x_mid", [P, TILES, H])
        norm2 = sb("norm2", [P, TILES, H])
        result = sb("result", [P, TILES, H])
        hidden = sb("hidden", [P, 2, TOK])
        hid_hi = sb("hid_hi", [P, FC, TOK], F32R)
        hid_lo = sb("hid_lo", [P, FC, TOK], F32R)
        stats1 = sb("stats1", [P, TILES, 6])
        stats2 = sb("stats2", [P, TILES, 6])
        moments1 = sb("moments1", [P, TILES, 2])
        moments2 = sb("moments2", [P, TILES, 2])
        var1 = sb("var1", [P, TILES])
        var2 = sb("var2", [P, TILES])
        rstd1 = sb("rstd1", [P, TILES])
        rstd2 = sb("rstd2", [P, TILES])

        raw = {
            "wq": probs[:, 0].rearrange("p a b -> p (a b)").rearrange("p (c n) -> p c n", c=KC),
            "wk": probs[:, 1].rearrange("p a b -> p (a b)").rearrange("p (c n) -> p c n", c=KC),
            "wv": probs[:, 2].rearrange("p a b -> p (a b)").rearrange("p (c n) -> p c n", c=KC),
            "wo": probs[:, 3].rearrange("p a b -> p (a b)").rearrange("p (c n) -> p c n", c=KC),
            "w1": probs_t[:, 0:4].rearrange("p a b -> p (a b)").rearrange("p (c n) -> p c n", c=KC),
            "w2": probs_t[:, 4:8].rearrange("p a b -> p (a b)").rearrange("p (c n) -> p c n", c=FC),
        }
        G1, BE1, G2, BE2, BQ, BK, BV, B1 = 0, 2, 4, 6, 8, 10, 12, 14

        score_bank = [psum(f"score_bank{i}") for i in range(2)]
        pt_bank = [psum(f"pt_bank{i}") for i in range(2)]
        pv_bank = psum("pv_bank")
        dense = [psum(f"dense{i}") for i in range(DENSE_BANKS)]

        consts_in = sem("consts_in")
        passed = sem("passed")
        w_in = {name: sem(f"{name}_in") for name in split}
        ident_ready, half_ready = sem("ident_ready"), sem("half_ready")
        bias_mm, biases_ready, bv_ready, bv_spread = (
            sem("bias_mm"), sem("biases_ready"), sem("bv_ready"), sem("bv_spread"))
        hi_by_dve, hi_by_act, weights_split = sem("hi_by_dve"), sem("hi_by_act"), sem("weights_split")
        x_ln1_in, x_mid_in, adj_in = sem("x_ln1_in"), sem("x_mid_in"), sem("adj_in")
        stats1_step, moments1_ready, var1_ready, rstd1_ready = (
            sem("stats1_step"), sem("moments1_ready"), sem("var1_ready"), sem("rstd1_ready"))
        stats2_step, moments2_ready, var2_ready, rstd2_ready = (
            sem("stats2_step"), sem("moments2_ready"), sem("var2_ready"), sem("rstd2_ready"))
        norm1_ready, norm2_ready = sem("norm1_ready"), sem("norm2_ready")
        norm1_hi_ready, norm2_hi_ready = sem("norm1_hi_ready"), sem("norm2_hi_ready")
        proj_hi_ready = sem("proj_hi_ready")
        stacked = [sem(f"stacked{pair}") for pair in range(HEADS // 2)]
        mask_ready = sem("mask_ready")
        scores_ready, max_ready, probs_ready = sem("scores_ready"), sem("max_ready"), sem("probs_ready")
        pt_filled, pt_by_act, pt_by_dve = sem("pt_filled"), sem("pt_by_act"), sem("pt_by_dve")
        inv_ready, wide_ready = sem("inv_ready"), sem("wide_ready")
        pv_done, attn_ready, attn_hi_ready, attn_lo_by_pool, attn_lo_by_dve = (
            sem("pv_done"), sem("attn_ready"), sem("attn_hi_ready"), sem("attn_lo_by_pool"), sem("attn_lo_by_dve"))
        x_biased, result_seeded = sem("x_biased"), sem("result_seeded")
        hid_hi_ready, hid_lo_by_pool, hid_lo_by_dve = (
            sem("hid_hi_ready"), sem("hid_lo_by_pool"), sem("hid_lo_by_dve"))
        stored = sem("stored")
        filled = [sem(f"filled{i}") for i in range(DENSE_BANKS)]
        read = [sem(f"read{i}") for i in range(DENSE_BANKS)]

        def run(engine, body):
            lo, hi = plan.looped
            for j in range(lo):
                body(j)
            with engine.Fori(lo, hi) as j:
                body(j)
            for j in range(hi, G + 2):
                body(j)

        def carried(engine):
            engine.sem_inc(passed, 1)

        def wait_filled(engine, j, unit, back=0):
            wait(engine, filled[plan.bank(unit)], plan.uses(j, unit, back))

        def wait_free(engine, j, unit):
            wait(engine, read[plan.bank(unit)], plan.uses(j, unit) - 1)

        def wait_read(engine, j, unit, back=0):
            wait(engine, read[plan.bank(unit)], plan.uses(j, unit, back))

        def bank_of(unit):
            return dense[plan.bank(unit)]

        def chunks_of(unit):
            return bank_of(unit)[:].rearrange("p (k s) -> p k s", k=KC)

        def hid_lo_count(group, f):
            ready = (hid_lo_by_pool, hid_lo_by_dve)[f % 2]
            return ready, FC // 2 * group + f // 2 + 1

        def fill_stack(engine, c):
            for g in range(4):
                for r, parts in enumerate((slice(0, 3, 2), slice(0, 4, 3), slice(1, 3, 1), slice(1, 4, 2))):
                    engine.dma_start(stack[HD * r:HD * r + HD, :, 4 * c + g].bitcast(F32),
                                     proj[HD * g:HD * g + HD, c, parts].bitcast(F32)
                                     ).then_inc(stacked[2 * c + g // 2], 16)

        block = ctx.enter_context(nc.Block())

        @block.sync
        def _(sp):
            sp.dma_start(norm1[:], x_dram[:, 0:TILES]).then_inc(x_ln1_in, 16)
            sp.dma_start(cols[:], columns).then_inc(consts_in, 16)
            sp.dma_start(bo_all[:], bo_row.partition_broadcast(P)).then_inc(consts_in, 16)
            sp.dma_start(b2_all[:], b2_row.partition_broadcast(P)).then_inc(consts_in, 16)
            for name, w in (("wq", wq), ("wk", wk), ("wv", wv), ("wo", wo), ("w1", w1), ("w2", w2)):
                sp.dma_start(raw[name], w.rearrange("(c p) n -> p c n", p=P)).then_inc(w_in[name], 16)

            def body(j):
                if plan.has(j, 1):
                    wait(sp, norm2_ready, TILES * (j - 1))
                    carried(sp)
                    wait(sp, result_seeded, j - 1)
                    carried(sp)
                    sp.dma_start(x_mid[:], x_dram[:, bass.ds((j - 1) * TILES, TILES)]).then_inc(x_mid_in, 16)
                if plan.has(j, 0):
                    wait(sp, mask_ready, j)
                    carried(sp)
                    sp.dma_start(adj_u8[:], adj_dram[:, bass.ds(j * TILES, TILES)]).then_inc(adj_in, 16)
                if plan.has(j, 2):
                    for u in range(GB):
                        wait_read(sp, j, f"W2_{u}")
                        carried(sp)
                        sp.dma_start(out_dram[:, bass.ds((j - 2) * TILES + QT * u, QT)],
                                     result[:, QT * u:QT * u + QT]).then_inc(stored, 16)
                if plan.has(j, -1):
                    wait_filled(sp, j, "LN1T1")
                    carried(sp)
                    sp.dma_start(norm1[:], x_dram[:, bass.ds((j + 1) * TILES, TILES)]).then_inc(x_ln1_in, 16)
                if plan.has(j, 0):
                    wait(sp, scores_ready, STEPS * j)
                    carried(sp)
                    for c in range(KC):
                        wait_read(sp, j, f"QK{2 * c}")
                        carried(sp)
                        wait_read(sp, j, f"QK{2 * c + 1}")
                        carried(sp)
                        fill_stack(sp, c)

            run(sp, body)
            sp.wait_ge(stored, 16 * GB * G)

        @block.tensor
        def _(pe):
            def beta_products(bank, names, beta):
                column = 0
                for name in names:
                    pe.wait_ge(w_in[name], 16)
                    for m in range(split[name][0].shape[2] // P):
                        for k in range(KC):
                            last = pe.matmul(bank[:, column:column + 1], raw[name][:, k, P * m:P * m + P],
                                             cols[:, beta + k:beta + k + 1], start=(k == 0), stop=(k == KC - 1))
                        column += 1
                last.then_inc(bias_mm, 1)

            pe.wait_ge(consts_in, 16 * 3)
            beta_products(pv_bank, ("wq", "wk"), BE1)
            pe.wait_ge(ident_ready, 2)

            def three(bank, lhs, rhs, chunks, release=None):
                for c in chunks:
                    for n, (a, b) in enumerate(((0, 0), (0, 1), (1, 0))):
                        last = pe.matmul(bank, lhs(a, c), rhs(b, c), start=(c == 0 and n == 0),
                                         stop=(c == KC - 1 and n == 2))
                if release is not None and KC - 1 in chunks:
                    last.then_inc(release, 1)

            ln1 = (norm1_hi, norm1_lo)
            ln2 = (norm2_hi, norm2_lo)
            att = (attn_hi, attn_lo)
            hid = (hid_hi, hid_lo)

            def scores(a, t):
                b, h = t // HEADS, t % HEADS
                if t in (0, 2, 4, 6):
                    wait(pe, stacked[t // 2], 16 * STACK_DMAS * (a + 1))
                wait(pe, max_ready, 2 * (STEPS * a + t - 1))
                for q in range(QT):
                    last = pe.matmul(score_bank[t % 2][:, S * q:S * q + S],
                                     stack[:, 0, h, S * b + P * q:S * b + P * q + P],
                                     stack[:, 1, h, S * b:S * b + S], start=True, stop=True)
                last.then_inc(scores_ready, 1)

            def turn(j, t):
                a = j - 1
                wait(pe, probs_ready, 2 * (STEPS * a + t + 1))
                before, turns = (t - 2, a) if t >= 2 else (t - 2 + STEPS, a - 1)
                if before in COPIED_BY_ACT:
                    wait(pe, pt_by_act, turns * copied(STEPS - 1, True) + copied(before, True))
                else:
                    wait(pe, pt_by_dve, turns * copied(STEPS - 1, False) + copied(before, False))
                for k in range(QT):
                    for q in range(QT):
                        last = pe.transpose(pt_bank[t % 2][:, S * k + P * q:S * k + P * q + P],
                                            probs[:, t % 4, q, P * k:P * k + P], ident[:])
                last.then_inc(pt_filled, 1)

            def values(j, quad):
                a, b, c = j - 1, quad // KC, quad % KC
                if quad == 0:
                    wait_read(pe, j, "V0", back=1)
                    wait_read(pe, j, "V1", back=1)
                last_step = 4 * quad + 3
                wait(pe, pt_by_act, a * copied(STEPS - 1, True) + copied(last_step, True))
                wait(pe, pt_by_dve, a * copied(STEPS - 1, False) + copied(last_step, False))
                wait(pe, attn_ready, QUADS * a + quad)
                for k in range(QT):
                    for g in range(4):
                        h = 4 * c + g
                        last = pe.matmul(pv_bank[HD * g:HD * g + HD, S * (quad % 2):S * (quad % 2) + S],
                                         v_nat[:, b, k, HD * h:HD * h + HD],
                                         probs_t[:, (4 * quad + g) % 8, S * k:S * k + S],
                                         start=(k == 0), stop=(k == QT - 1))
                last.then_inc(pv_done, 1)

            def turn_inverse(j, quad):
                unit = f"RT{quad}"
                wait(pe, wide_ready, QUADS * (j - 1) + quad + 1)
                wait_free(pe, j, unit)
                for q in range(QT):
                    last = pe.transpose(bank_of(unit)[:, P * q:P * q + P],
                                        inv_wide[:, q].rearrange("p g d -> p (g d)"), ident[:])
                last.then_inc(filled[plan.bank(unit)], 1)

            def mlp_out(j, n):
                half, piece, u = n // (2 * FC), n // 2 % FC, n % 2
                unit, tile = f"W2_{half}", QT * half + u
                if piece == 0 and u == 0:
                    wait_free(pe, j, unit)
                if half == 0 and u == 0:
                    lo_ready, count = hid_lo_count(j - 2, piece)
                    wait(pe, hid_hi_ready, FC * (j - 2) + piece + 1)
                    wait(pe, lo_ready, count)
                for i, (a, b) in enumerate(((0, 0), (0, 1), (1, 0))):
                    last = pe.matmul(bank_of(unit)[:, H * u:H * u + H], hid[a][:, piece, P * tile:P * tile + P],
                                     split["w2"][b][:, piece, :], start=(piece == 0 and u == 0 and i == 0),
                                     stop=(piece == FC - 1 and i == 2), skip_group_check=True)
                if piece == FC - 1 and u == QT - 1:
                    last.then_inc(filled[plan.bank(unit)], 1)

            def turn_norm1(j, k):
                unit = f"LN1T{k}"
                wait_free(pe, j, unit)
                wait(pe, norm1_ready, TILES * (j + 1))
                for t in range(TILES):
                    last = pe.transpose(bank_of(unit)[:, P * t:P * t + P], norm1[:, t, P * k:P * k + P], ident[:])
                last.then_inc(filled[plan.bank(unit)], 1)

            def turn_norm2(j, b):
                unit = f"LN2T{b}"
                wait_free(pe, j, unit)
                for t in range(QT * b, QT * b + QT):
                    wait(pe, norm2_ready, TILES * (j - 1) + t + 1)
                    for k in range(KC):
                        last = pe.transpose(bank_of(unit)[:, S * k + P * (t % QT):S * k + P * (t % QT) + P],
                                            norm2[:, t, P * k:P * k + P], ident[:])
                last.then_inc(filled[plan.bank(unit)], 1)

            def project(j, m, chunks=range(KC)):
                unit, w, c = f"QK{m}", split["wk" if m % 2 else "wq"], m // 2
                if m == 0:
                    wait_read(pe, j, "LN1T0")
                    wait_read(pe, j, "LN1T1")
                if 0 in chunks:
                    wait_free(pe, j, unit)
                three(bank_of(unit)[:], lambda a, k: w[a][:, k, P * c:P * c + P], lambda b, k: ln1[b][:, k, :],
                      chunks, filled[plan.bank(unit)])

            def project_v(j, b):
                unit = f"V{b}"
                wait_free(pe, j, unit)
                for t in range(QT):
                    tile = QT * b + t
                    three(bank_of(unit)[:, H * t:H * t + H], lambda a, k: ln1[a][:, k, P * tile:P * tile + P],
                          lambda c, k: split["wv"][c][:, k, :], range(KC),
                          filled[plan.bank(unit)] if t == QT - 1 else None)

            def project_out(j, b):
                unit = f"Wo{b}"
                done = QUADS * (j - 1) + KC * (b + 1)
                wait(pe, attn_hi_ready, done)
                wait(pe, (attn_lo_by_pool, attn_lo_by_dve)[b], KC * j)
                wait_free(pe, j, unit)
                for t in range(QT):
                    tile = QT * b + t
                    three(bank_of(unit)[:, H * t:H * t + H], lambda a, k: att[a][:, k, P * tile:P * tile + P],
                          lambda c, k: split["wo"][c][:, k, :], range(KC),
                          filled[plan.bank(unit)] if t == QT - 1 else None)

            def mlp_in(j, f):
                unit, w = f"W1_{f}", split["w1"]
                if f == 0:
                    wait(pe, norm2_hi_ready, GB * j)
                wait_free(pe, j, unit)
                for n, (a, b, k) in enumerate([(a, 0, k) for k in range(KC) for a in (0, 1)] +
                                              [(0, 1, k) for k in range(KC)]):
                    if f == 0 and n == 2 * KC:
                        wait_read(pe, j, "LN2T0")
                        wait_read(pe, j, "LN2T1")
                    last = pe.matmul(bank_of(unit)[:], w[a][:, k, P * f:P * f + P], ln2[b][:, k, :],
                                     start=(n == 0), stop=(n == 3 * KC - 1))
                last.then_inc(filled[plan.bank(unit)], 1)

            def body(j):
                now, before, two_before = plan.has(j, 0), plan.has(j, 1), plan.has(j, 2)
                if isinstance(j, int) and j == 0:
                    pe.wait_ge(weights_split, 3)
                if isinstance(j, int) and j == 1:
                    pe.wait_ge(biases_ready, 3)
                    pe.wait_ge(weights_split, 6)
                n = 0
                for t in range(STEPS):
                    if before and 2 <= t < STEPS - 2:
                        scores(j - 1, t + 2)
                    for i in range(MLP_UNITS[t]):
                        if i == MLP_UNITS[t] // 2 and before and t >= 2:
                            turn(j, t - 2)
                        if two_before:
                            mlp_out(j, n)
                        n += 1
                    if t == 12 and isinstance(j, int) and j == 0:
                        beta_products(score_bank[0], ("wv",), BE1)
                    if now and t in (10, 13):
                        turn_norm1(j, (t - 10) // 3)
                    if before and t % 4 == 3 and t > 3:
                        turn_inverse(j, (t - 7) // 4)
                        values(j, (t - 7) // 4)
                if before:
                    turn(j, 14)
                if now:
                    project(j, 0)
                if before:
                    turn(j, 15)
                if now:
                    project(j, 1)
                if before:
                    turn_inverse(j, 3)
                    values(j, 3)
                    project_out(j, 0)
                if now:
                    project(j, 2)
                if before:
                    project_out(j, 1)
                if now:
                    project_v(j, 0)
                    project_v(j, 1)
                    project(j, 3, (0,))
                if before:
                    turn_norm2(j, 0)
                    turn_norm2(j, 1)
                if now:
                    project(j, 3, (1,))
                if isinstance(j, int) and j == 0:
                    beta_products(pt_bank[0], ("w1",), BE2)
                    pe.wait_ge(w_in["wo"], 16)
                    pe.wait_ge(bv_spread, 1)
                    for k in range(KC):
                        last = pe.matmul(pt_bank[1][:, 0:H], inv_t[:, 0, P * k:P * k + P], raw["wo"][:, k, :],
                                         start=(k == 0), stop=(k == KC - 1))
                    last.then_inc(bias_mm, 1)
                if now:
                    scores(j, 0)
                    scores(j, 1)
                for f in range(FC):
                    if now and f >= FC - 2:
                        scores(j, f - (FC - 2) + 2)
                    if before:
                        mlp_in(j, f)

            run(pe, body)

        @block.scalar
        def _(act):
            act.wait_ge(w_in["wo"], 16)
            nc.scalar.copy(split["wo"][0][:], raw["wo"]).then_inc(hi_by_act, 1)

            def exps(j, t):
                a = j - 1
                for q in range(QT):
                    wait(act, max_ready, 2 * (STEPS * a + t) + q + 1)
                    nc.scalar.activation(probs[:, t % 4, q, :], probs[:, t % 4, q, :], ACT.Exp,
                                         bias=neg_max[:, t, q:q + 1], scale=-1.0,
                                         accum_out=row_sum[:, t, q:q + 1]).then_inc(probs_ready, 1)

            def copy_turned(j, t):
                if t not in COPIED_BY_ACT:
                    return
                a = j - 1
                wait(act, pt_filled, STEPS * a + t + 1)
                wait(act, pv_done, QUADS * a + t // 4 - 1)
                nc.scalar.copy(probs_t[:, t % 8, :], pt_bank[t % 2][:]).then_inc(pt_by_act, 1)

            def copy_inverse(j, quad):
                unit = f"RT{quad}"
                wait_filled(act, j, unit)
                wait(act, attn_ready, QUADS * (j - 1) + quad - 1)
                nc.scalar.copy(inv_t[:, quad % 2, :], bank_of(unit)[:, 0:S]).then_inc(read[plan.bank(unit)], 1)

            def split_attn(j, quad):
                b, c = quad // KC, quad % KC
                if quad == 0 and plan.has(j, 2):
                    wait_filled(act, j, "W1_7", back=1)
                wait(act, attn_ready, QUADS * (j - 1) + quad + 1)
                nc.scalar.copy(attn_hi[:, c, S * b:S * b + S], attn[:, quad % 2, :]).then_inc(attn_hi_ready, 1)

            def split_norm1(j, k):
                wait_filled(act, j, f"LN1T{k}")
                if k == 0 and plan.has(j, 1):
                    wait_filled(act, j, "QK3", back=1)
                nc.scalar.copy(norm1_hi[:, k, :], bank_of(f"LN1T{k}")[:]).then_inc(norm1_hi_ready, 1)

            def split_norm2(j, b):
                wait_filled(act, j, f"LN2T{b}")
                if b == 0:
                    wait_filled(act, j, "Wo1")
                nc.scalar.copy(norm2_hi[:, :, S * b:S * b + S], chunks_of(f"LN2T{b}")).then_inc(norm2_hi_ready, 1)

            def split_proj(j, m):
                unit = f"QK{m}"
                wait_filled(act, j, unit)
                if m % 2 == 0:
                    wait(act, stacked[m], 16 * STACK_DMAS * j)
                    wait(act, stacked[m + 1], 16 * STACK_DMAS * j)
                nc.scalar.activation(proj[:, m // 2, 2 * (m % 2), :], bank_of(unit)[:], ACT.Identity,
                                     bias=qk_bias[:, 2 * (m % 2) + m // 2:2 * (m % 2) + m // 2 + 1],
                                     scale=1.0).then_inc(proj_hi_ready, 1)

            def copy_v(j, b):
                unit = f"V{b}"
                wait_filled(act, j, unit)
                wait(act, pv_done, QUADS * j)
                nc.scalar.copy(v_nat[:, b].rearrange("p t h -> p (t h)"),
                               bank_of(unit)[:]).then_inc(read[plan.bank(unit)], 1)

            def gelu(j, f):
                unit = f"W1_{f}"
                wait_filled(act, j, unit)
                lo_ready, count = hid_lo_count(j - 1, f)
                wait(act, lo_ready, count - 1)
                nc.scalar.activation(hidden[:, f % 2, :], bank_of(unit)[:], ACT.Gelu, bias=b1_col[:, f:f + 1],
                                     scale=1.0).then_inc(read[plan.bank(unit)], 1)

            def body(j):
                now, before = plan.has(j, 0), plan.has(j, 1)
                if isinstance(j, int) and j == 0:
                    act.wait_ge(biases_ready, 1)
                for t in range(STEPS):
                    if before:
                        if t == 0 and isinstance(j, int) and j == 1:
                            act.wait_ge(biases_ready, 3)
                        exps(j, t)
                        if t >= 2:
                            copy_turned(j, t - 2)
                        if t in (9, 13):
                            split_attn(j, (t - 9) // 4)
                        if t % 4 == 3 and t > 3:
                            copy_inverse(j, (t - 7) // 4)
                    if now and t in (11, 14):
                        split_norm1(j, (t - 11) // 3)
                if before:
                    copy_turned(j, 14)
                    split_attn(j, 2)
                    copy_turned(j, 15)
                if now:
                    split_proj(j, 0)
                    split_proj(j, 1)
                if before:
                    copy_inverse(j, 3)
                    split_attn(j, 3)
                if now:
                    split_proj(j, 2)
                    copy_v(j, 0)
                    copy_v(j, 1)
                if before:
                    split_norm2(j, 0)
                    split_norm2(j, 1)
                if now:
                    split_proj(j, 3)
                if isinstance(j, int) and j == 0:
                    act.wait_ge(w_in["w2"], 16)
                    nc.scalar.copy(split["w2"][0][:], raw["w2"]).then_inc(hi_by_act, 1)
                if before:
                    for f in range(FC):
                        gelu(j, f)

            run(act, body)

        @block.vector
        def _(dve):
            def split_weight(number, name, gain):
                hi, lo = split[name]
                dve.wait_ge(w_in[name], 16)
                for k in range(KC):
                    nc.vector.tensor_scalar(hi[:, k, :], raw[name][:, k, :], cols[:, gain + k:gain + k + 1], None,
                                            ALU.mult).then_inc(hi_by_dve, 1)
                for k in range(KC):
                    dve.wait_ge(hi_by_dve, KC * number + k + 1)
                    last = nc.vector.scalar_tensor_tensor(
                        out=lo[:, k, :], in0=raw[name][:, k, :], scalar=cols[:, gain + k:gain + k + 1],
                        in1=hi[:, k, :].bitcast(F32), op0=ALU.mult, op1=ALU.subtract)
                last.then_inc(weights_split, 1)

            def row_moments(stats, step, moments, ready, first, tiles, group):
                for t in range(first, first + tiles):
                    wait(dve, step, TILES * group + t + 1)
                    carried(dve)
                    last = nc.vector.bn_aggr(moments[:, t, :], stats[:, t, :])
                last.then_inc(ready, 1)

            def ln1_statistics(group, t):
                if t == 0:
                    wait(dve, x_ln1_in, 16 * (group + 1))
                nc.vector.bn_stats(stats1[:, t, :], norm1[:, t, :]).then_inc(stats1_step, 1)
                if t == TILES - 1:
                    row_moments(stats1, stats1_step, moments1, moments1_ready, 0, TILES, group)

            def ln2_normalise(j, b):
                for t in range(QT * b, QT * b + QT):
                    wait(dve, rstd2_ready, GB * (j - 1) + t // QT + 1)
                    nc.vector.tensor_scalar(norm2[:, t, :], x_mid[:, t, :], moments2[:, t, 0:1], rstd2[:, t:t + 1],
                                            ALU.subtract, ALU.mult).then_inc(norm2_ready, 1)

            def maxima(a, t):
                b = t // HEADS
                if t == 0:
                    wait(dve, mask_ready, a + 1)
                wait(dve, scores_ready, STEPS * a + t + 1)
                wait(dve, pt_filled, STEPS * a + t - 3)
                carried(dve)
                for q in range(QT):
                    nc.vector.tensor_tensor_reduce(
                        probs[:, t % 4, q, :], score_bank[t % 2][:, S * q:S * q + S], mask_add[:, QT * b + q, :],
                        -SCALE, HUGE, ALU.add, ALU.min, neg_max[:, t, q:q + 1]).then_inc(max_ready, 1)

            def copy_turned(j, t):
                if t in COPIED_BY_ACT:
                    return
                a = j - 1
                wait(dve, pt_filled, STEPS * a + t + 1)
                wait(dve, pv_done, QUADS * a + t // 4 - 1)
                nc.vector.tensor_copy(probs_t[:, t % 8, :], pt_bank[t % 2][:]).then_inc(pt_by_dve, 1)

            def invert(j, quad):
                a = j - 1
                wait(dve, wide_ready, QUADS * a + quad)
                wait(dve, probs_ready, 2 * (STEPS * a + 4 * quad + 4))
                nc.vector.reciprocal(row_inv[:], row_sum[:, 4 * quad:4 * quad + 4, :]).then_inc(inv_ready, 1)
                if quad > 0:
                    wait_filled(dve, j, f"RT{quad - 1}")
                wait(dve, inv_ready, QUADS * a + quad + 1)
                nc.vector.tensor_copy(inv_wide[:], row_inv[:].rearrange("p g q -> p q g").unsqueeze(3)
                                      .broadcast_to([P, QT, 4, HD])).then_inc(wide_ready, 1)

            def normalise(j, quad):
                wait(dve, pv_done, QUADS * (j - 1) + quad + 1)
                wait_read(dve, j, f"RT{quad}")
                wait(dve, attn_hi_ready, QUADS * (j - 1) + quad - 1)
                if quad in (2, 3):
                    wait(dve, attn_lo_by_pool, KC * (j - 1) + quad - 1)
                nc.vector.tensor_tensor(attn[:, quad % 2, :], pv_bank[:, S * (quad % 2):S * (quad % 2) + S],
                                        inv_t[:, quad % 2, :], ALU.mult).then_inc(attn_ready, 1)

            def split_attn(j, quad):
                b, c = quad // KC, quad % KC
                wait(dve, attn_ready, QUADS * (j - 1) + quad + 1)
                wait(dve, attn_hi_ready, QUADS * (j - 1) + quad + 1)
                nc.vector.tensor_tensor(attn_lo[:, c, S * b:S * b + S], attn[:, quad % 2, :],
                                        attn_hi[:, c, S * b:S * b + S].bitcast(F32),
                                        ALU.subtract).then_inc(attn_lo_by_dve, 1)

            def split_norm1(j, k):
                unit = f"LN1T{k}"
                wait(dve, norm1_hi_ready, KC * j + k + 1)
                nc.vector.tensor_tensor(norm1_lo[:, k, :], bank_of(unit)[:], norm1_hi[:, k, :].bitcast(F32),
                                        ALU.subtract).then_inc(read[plan.bank(unit)], 1)

            def split_norm2(j, b):
                unit = f"LN2T{b}"
                wait(dve, norm2_hi_ready, GB * (j - 1) + b + 1)
                nc.vector.tensor_tensor(norm2_lo[:, :, S * b:S * b + S], chunks_of(unit),
                                        norm2_hi[:, :, S * b:S * b + S].bitcast(F32),
                                        ALU.subtract).then_inc(read[plan.bank(unit)], 1)

            def split_proj(j, m):
                unit = f"QK{m}"
                wait(dve, proj_hi_ready, 4 * j + m + 1)
                nc.vector.scalar_tensor_tensor(
                    out=proj[:, m // 2, 2 * (m % 2) + 1, :], in0=bank_of(unit)[:],
                    scalar=qk_bias[:, 2 * (m % 2) + m // 2:2 * (m % 2) + m // 2 + 1],
                    in1=proj[:, m // 2, 2 * (m % 2), :].bitcast(F32), op0=ALU.add,
                    op1=ALU.subtract).then_inc(read[plan.bank(unit)], 1)

            def add_attention(j, b):
                unit = f"Wo{b}"
                wait(dve, x_biased, j)
                wait_filled(dve, j, unit)
                tiles = x_mid[:, QT * b:QT * b + QT, :].rearrange("p t h -> p (t h)")
                nc.vector.tensor_tensor(tiles, bank_of(unit)[:], tiles, ALU.add).then_inc(read[plan.bank(unit)], 1)
                wait_read(dve, j, unit)
                for t in range(QT * b, QT * b + QT):
                    nc.vector.bn_stats(stats2[:, t, :], x_mid[:, t, :]).then_inc(stats2_step, 1)
                row_moments(stats2, stats2_step, moments2, moments2_ready, QT * b, QT, j - 1)

            def add_mlp(j, half):
                unit = f"W2_{half}"
                wait(dve, result_seeded, j - 1)
                wait_filled(dve, j, unit)
                tiles = result[:, QT * half:QT * half + QT, :].rearrange("p t h -> p (t h)")
                nc.vector.tensor_tensor(tiles, bank_of(unit)[:], tiles, ALU.add).then_inc(read[plan.bank(unit)], 1)

            def round_hidden(j, f):
                wait_read(dve, j, f"W1_{f}")
                nc.vector.tensor_copy(hid_hi[:, f, :], hidden[:, f % 2, :]).then_inc(hid_hi_ready, 1)
                if f % 2 == 1:
                    wait(dve, hid_hi_ready, FC * (j - 1) + f + 1)
                    nc.vector.tensor_tensor(hid_lo[:, f, :], hidden[:, f % 2, :], hid_hi[:, f, :].bitcast(F32),
                                            ALU.subtract).then_inc(hid_lo_by_dve, 1)

            def body(j):
                now, before, two_before = (plan.has(j, back) for back in (0, 1, 2))
                for t in range(STEPS):
                    if before:
                        if 2 <= t < STEPS - 2:
                            maxima(j - 1, t + 2)
                        if t >= 2:
                            copy_turned(j, t - 2)
                        if t % 4 == 1 and t > 1:
                            invert(j, (t - 5) // 4)
                        if t % 4 == 0 and t > 4:
                            normalise(j, (t - 8) // 4)
                    if now and t in (11, 14):
                        split_norm1(j, (t - 11) // 3)
                    if two_before and t == 7:
                        add_mlp(j, 0)
                if before:
                    invert(j, 3)
                    copy_turned(j, 14)
                if two_before:
                    add_mlp(j, 1)
                if before:
                    normalise(j, 2)
                if now:
                    split_proj(j, 0)
                if before:
                    split_attn(j, 2)
                    copy_turned(j, 15)
                if now:
                    split_proj(j, 1)
                if isinstance(j, int) and j == 0:
                    split_weight(3, "w1", G2)
                if before:
                    normalise(j, 3)
                    split_attn(j, 3)
                    add_attention(j, 0)
                if now:
                    split_proj(j, 2)
                if before:
                    add_attention(j, 1)
                    ln2_normalise(j, 0)
                    ln2_normalise(j, 1)
                    split_norm2(j, 0)
                    split_norm2(j, 1)
                if now:
                    split_proj(j, 3)
                if isinstance(j, int) and j == 0:
                    dve.wait_ge(bias_mm, 2)
                    nc.vector.tensor_tensor(bv_col[:], score_bank[0][:, 0:KC], cols[:, BV:BV + KC],
                                            ALU.add).then_inc(bv_ready, 1)
                    dve.wait_ge(bv_ready, 1)
                    nc.vector.tensor_copy(inv_t[:, 0, :].rearrange("p (k m) -> p k m", k=KC),
                                          bv_col[:].unsqueeze(2).broadcast_to([P, KC, P])).then_inc(bv_spread, 1)
                    dve.wait_ge(bias_mm, 3)
                    nc.vector.tensor_tensor(b1_col[:], pt_bank[0][:, 0:FC], cols[:, B1:B1 + FC],
                                            ALU.add).then_inc(biases_ready, 1)
                    dve.wait_ge(bias_mm, 4)
                    nc.vector.tensor_tensor(bo_all[:], pt_bank[1][:, 0:H], bo_all[:], ALU.add).then_inc(biases_ready, 1)
                    dve.wait_ge(weights_split, 5)
                if now:
                    maxima(j, 0)
                    maxima(j, 1)
                for f in range(FC):
                    if before:
                        round_hidden(j, f)
                    if plan.has(j, -1) and 1 <= f <= TILES:
                        ln1_statistics(j + 1, f - 1)
                    if now and f >= FC - 2:
                        maxima(j, f - (FC - 2) + 2)

            for t in range(TILES):
                ln1_statistics(0, t)
            dve.wait_ge(consts_in, 16 * 3)
            split_weight(0, "wq", G1)
            dve.wait_ge(rstd1_ready, 1)
            for t in range(TILES):
                nc.vector.tensor_scalar(norm1[:, t, :], norm1[:, t, :], moments1[:, t, 0:1], rstd1[:, t:t + 1],
                                        ALU.subtract, ALU.mult).then_inc(norm1_ready, 1)
            split_weight(1, "wk", G1)
            split_weight(2, "wv", G1)
            dve.wait_ge(bias_mm, 1)
            nc.vector.tensor_tensor(qk_bias[:], pv_bank[:, 0:4], cols[:, BQ:BQ + 4], ALU.add).then_inc(biases_ready, 1)
            run(dve, body)

        @block.gpsimd
        def _(pool):
            nc.gpsimd.memset(neg_half[:], -0.5).then_inc(half_ready, 1)
            nc.gpsimd.memset(ident[:], 0.0).then_inc(ident_ready, 1)
            pool.wait_ge(ident_ready, 1)
            nc.gpsimd.affine_select(out=ident[:], in_=ident[:], compare_op=ALU.not_equal, fill=1.0, base=0,
                                    pattern=[[-1, P]], channel_multiplier=1).then_inc(ident_ready, 1)
            pool.wait_ge(half_ready, 1)

            def inverse_deviation(moments, var, var_ready, rstd, ready, first, count, number):
                tiles = slice(first, first + count)
                carried(pool)
                nc.gpsimd.tensor_scalar(var[:, tiles], moments[:, tiles, 1], LN_EPS, 1.0, ALU.add,
                                        ALU.mult).then_inc(var_ready, 1)
                wait(pool, var_ready, number)
                nc.gpsimd.tensor_tensor(rstd[:, tiles], var[:, tiles], neg_half[:, tiles], ALU.pow).then_inc(ready, 1)

            def split_attn(j, c):
                wait(pool, attn_hi_ready, QUADS * (j - 1) + c + 1)
                nc.gpsimd.tensor_tensor(attn_lo[:, c, 0:S], attn[:, c, :], attn_hi[:, c, 0:S].bitcast(F32),
                                        ALU.subtract).then_inc(attn_lo_by_pool, 1)

            def body(j):
                now, before, two_before = (plan.has(j, back) for back in (0, 1, 2))
                if two_before:
                    wait(pool, stored, 16 * GB * (j - 2))
                    nc.gpsimd.tensor_tensor(result[:], x_mid[:], b2_all[:].unsqueeze(1).broadcast_to([P, TILES, H]),
                                            ALU.add).then_inc(result_seeded, 1)
                if now:
                    wait(pool, moments1_ready, j + 1)
                    inverse_deviation(moments1, var1, var1_ready, rstd1, rstd1_ready, 0, TILES, j + 1)
                    wait(pool, rstd1_ready, j + 1)
                    carried(pool)
                    for t in range(TILES) if not (isinstance(j, int) and j == 0) else ():
                        nc.gpsimd.tensor_scalar(norm1[:, t, :], norm1[:, t, :], moments1[:, t, 0:1],
                                                rstd1[:, t:t + 1], ALU.subtract, ALU.mult).then_inc(norm1_ready, 1)
                if before:
                    if isinstance(j, int) and j == 1:
                        pool.wait_ge(biases_ready, 3)
                    wait(pool, x_mid_in, 16 * j)
                    nc.gpsimd.tensor_tensor(x_mid[:], x_mid[:], bo_all[:].unsqueeze(1).broadcast_to([P, TILES, H]),
                                            ALU.add).then_inc(x_biased, 1)
                    for c in range(KC):
                        split_attn(j, c)
                if now:
                    wait(pool, adj_in, 16 * (j + 1))
                    wait(pool, max_ready, 2 * STEPS * j)
                    carried(pool)
                    nc.gpsimd.tensor_scalar(mask_add[:], adj_u8[:], -1.0, MASKED, ALU.add,
                                            ALU.mult).then_inc(mask_ready, 1)
                if isinstance(j, int) and j == 0:
                    pool.wait_ge(weights_split, 4)
                    for number, name in enumerate(("wo", "w2")):
                        pool.wait_ge(hi_by_act, number + 1)
                        nc.gpsimd.tensor_tensor(split[name][1][:], raw[name], split[name][0][:].bitcast(F32),
                                                ALU.subtract).then_inc(weights_split, 1)
                if before:
                    for b in range(GB):
                        wait(pool, moments2_ready, GB * (j - 1) + b + 1)
                        inverse_deviation(moments2, var2, var2_ready, rstd2, rstd2_ready, QT * b, QT,
                                          GB * (j - 1) + b + 1)
                    for f in range(0, FC, 2):
                        wait(pool, hid_hi_ready, FC * (j - 1) + f + 1)
                        nc.gpsimd.tensor_tensor(hid_lo[:, f, :], hidden[:, f % 2, :], hid_hi[:, f, :].bitcast(F32),
                                                ALU.subtract).then_inc(hid_lo_by_pool, 1)

            run(pool, body)


def columns_of(*vectors):
    import numpy as np

    return np.ascontiguousarray(np.concatenate([v.reshape(-1, P).T for v in vectors], axis=1))


def kernel(x, adj, L0_gnn_ln1_g, L0_gnn_ln1_b, L0_gnn_ln2_g, L0_gnn_ln2_b, L0_gnn_Wq, L0_gnn_bq, L0_gnn_Wk,
           L0_gnn_bk, L0_gnn_Wv, L0_gnn_bv, L0_gnn_Wo, L0_gnn_bo, L0_gnn_W1, L0_gnn_b1, L0_gnn_W2, L0_gnn_b2):
    import numpy as np
    from concourse import bacc
    from concourse.bass_utils import run_bass_kernel_spmd

    columns = columns_of(*(np.asarray(v) for v in (
        L0_gnn_ln1_g, L0_gnn_ln1_b, L0_gnn_ln2_g, L0_gnn_ln2_b, L0_gnn_bq, L0_gnn_bk, L0_gnn_bv, L0_gnn_b1)))
    inputs = {
        "x": x, "adj": adj, "columns": columns,
        "bo_row": np.asarray(L0_gnn_bo), "b2_row": np.asarray(L0_gnn_b2),
        "wq": L0_gnn_Wq, "wk": L0_gnn_Wk, "wv": L0_gnn_Wv, "wo": L0_gnn_Wo, "w1": L0_gnn_W1, "w2": L0_gnn_W2,
    }
    nc = bacc.Bacc("TRN2", target_bir_lowering=False, num_devices=1)
    arrays, args = {}, []
    for name, a in inputs.items():
        a = np.ascontiguousarray(a)
        arrays[f"in_{name}"] = a
        args.append(nc.dram_tensor(f"in_{name}", a.shape, mybir.dt.from_np(a.dtype), kind="ExternalInput").ap())
    args.append(nc.dram_tensor("out", np.asarray(x).shape, F32, kind="ExternalOutput").ap())
    gnn_block(nc, *args)
    return run_bass_kernel_spmd(nc, [arrays], core_ids=[0]).results[0]["out"]
```
